# Optimizing a Trainium2 kernel written in Bass

```python
import numpy as np
import jax
import jax.numpy as jnp

def _softmax(x, axis=-1):
    return jax.nn.softmax(x, axis=axis)

def _gelu(x):
    return jax.nn.gelu(x, approximate=True)

def _silu(x):
    return jax.nn.silu(x)

def _sigmoid(x):
    return jax.nn.sigmoid(x)

def _layernorm(x, axis=-1, eps=1e-05):
    m = jnp.mean(x, axis=axis, keepdims=True)
    v = jnp.var(x, axis=axis, keepdims=True)
    return (x - m) / jnp.sqrt(v + eps)

def _scatter_add(tgt, idx, src, axis=0):
    return tgt.at[idx].add(src)

def _segment_sum(src, seg, n):
    return jax.ops.segment_sum(src, seg, n)
kernel_name = 'mk_conv_preact_d1_conv_nchw256_r2_446599'

def setup_inputs(seed: int=0):
    np.random.seed(seed)
    _w = jnp.asarray

    def _rec_inputs():
        import jax
        import jax.numpy as jnp
        _gk = jax.random.key(seed)
        x = 7.22e-05 + 1 * jax.random.normal(jax.random.fold_in(_gk, 1), (8, 128, 32, 32), jnp.float32)
        return x
    x = _rec_inputs()

    def _L0_conv_setup():
        import jax, jax.numpy as jnp
        import numpy as np
        from jax import lax
        B, C, H, W = (8, 128, 32, 32)

        def _conv1d(x, w, b):
            y = lax.conv_general_dilated(x, w, (1,), ((1, 1),), dimension_numbers=('NCH', 'OIH', 'NCH'))
            return y + b[None, :, None]

        def _gru_step(x, h, wih, whh):
            gi = x @ wih.T
            gh = h @ whh.T
            ir, iz, i_n = jnp.split(gi, 3, axis=-1)
            hr, hz, h_n = jnp.split(gh, 3, axis=-1)
            r = jax.nn.sigmoid(ir + hr)
            z = jax.nn.sigmoid(iz + hz)
            n = jnp.tanh(i_n + r * h_n)
            return (1.0 - z) * n + z * h

        def _direction(xs, wih, whh, cw, cb):
            T, b, c, L = xs.shape

            def step(h, xr):
                xi = xr.transpose(0, 2, 1).reshape(b * L, c)
                out = _gru_step(xi, h, wih, whh)
                ctx = out.reshape(b, L, c).transpose(0, 2, 1)
                h_new = jnp.tanh(_conv1d(ctx, cw, cb)).transpose(0, 2, 1).reshape(b * L, c)
                return (h_new, ctx)
            h0 = jnp.zeros((b * L, c), xs.dtype)
            _, ctxs = lax.scan(step, h0, xs)
            return ctxs
        key = jax.random.key(seed)
        ks = jax.random.split(key, 20)
        s = 1.0 / np.sqrt(C)
        d = {'x': jax.random.normal(ks[0], (B, C, H, W), jnp.float32)}
        names = ['d', 'u', 'l', 'r']
        for i, nm in enumerate(names):
            d[f'wih_{nm}'] = jax.random.normal(ks[1 + 4 * i], (3 * C, C), jnp.float32) * s
            d[f'whh_{nm}'] = jax.random.normal(ks[2 + 4 * i], (3 * C, C), jnp.float32) * s
            d[f'cw_{nm}'] = jax.random.normal(ks[3 + 4 * i], (C, C, 3), jnp.float32) * s
            d[f'cb_{nm}'] = jnp.zeros((C,), jnp.float32)
        d['w_comb'] = jax.random.normal(ks[17], (C, 4 * C), jnp.float32) * (1.0 / np.sqrt(4 * C))
        d['b_comb'] = jnp.zeros((C,), jnp.float32)
        return d
    _L0_conv_all = _L0_conv_setup()
    _L0_conv_in = {k: v for k, v in _L0_conv_all.items() if k in ('wih_d', 'whh_d', 'cw_d', 'cb_d', 'wih_u', 'whh_u', 'cw_u', 'cb_u', 'wih_l', 'whh_l', 'cw_l', 'cb_l', 'wih_r', 'whh_r', 'cw_r', 'cb_r', 'w_comb', 'b_comb')}
    del _L0_conv_all
    return {'x': x, 'L0_conv_wih_d': _L0_conv_in['wih_d'], 'L0_conv_whh_d': _L0_conv_in['whh_d'], 'L0_conv_cw_d': _L0_conv_in['cw_d'], 'L0_conv_cb_d': _L0_conv_in['cb_d'], 'L0_conv_wih_u': _L0_conv_in['wih_u'], 'L0_conv_whh_u': _L0_conv_in['whh_u'], 'L0_conv_cw_u': _L0_conv_in['cw_u'], 'L0_conv_cb_u': _L0_conv_in['cb_u'], 'L0_conv_wih_l': _L0_conv_in['wih_l'], 'L0_conv_whh_l': _L0_conv_in['whh_l'], 'L0_conv_cw_l': _L0_conv_in['cw_l'], 'L0_conv_cb_l': _L0_conv_in['cb_l'], 'L0_conv_wih_r': _L0_conv_in['wih_r'], 'L0_conv_whh_r': _L0_conv_in['whh_r'], 'L0_conv_cw_r': _L0_conv_in['cw_r'], 'L0_conv_cb_r': _L0_conv_in['cb_r'], 'L0_conv_w_comb': _L0_conv_in['w_comb'], 'L0_conv_b_comb': _L0_conv_in['b_comb']}

def reference(x, L0_conv_wih_d, L0_conv_whh_d, L0_conv_cw_d, L0_conv_cb_d, L0_conv_wih_u, L0_conv_whh_u, L0_conv_cw_u, L0_conv_cb_u, L0_conv_wih_l, L0_conv_whh_l, L0_conv_cw_l, L0_conv_cb_l, L0_conv_wih_r, L0_conv_whh_r, L0_conv_cw_r, L0_conv_cb_r, L0_conv_w_comb, L0_conv_b_comb):
    import jax
    import jax.numpy as jnp

    def _L0_conv_ref(x, wih_d, whh_d, cw_d, cb_d, wih_u, whh_u, cw_u, cb_u, wih_l, whh_l, cw_l, cb_l, wih_r, whh_r, cw_r, cb_r, w_comb, b_comb):
        import jax, jax.numpy as jnp
        import numpy as np
        from jax import lax
        B, C, H, W = (8, 128, 32, 32)

        def _conv1d(x, w, b):
            y = lax.conv_general_dilated(x, w, (1,), ((1, 1),), dimension_numbers=('NCH', 'OIH', 'NCH'))
            return y + b[None, :, None]

        def _gru_step(x, h, wih, whh):
            gi = x @ wih.T
            gh = h @ whh.T
            ir, iz, i_n = jnp.split(gi, 3, axis=-1)
            hr, hz, h_n = jnp.split(gh, 3, axis=-1)
            r = jax.nn.sigmoid(ir + hr)
            z = jax.nn.sigmoid(iz + hz)
            n = jnp.tanh(i_n + r * h_n)
            return (1.0 - z) * n + z * h

        def _direction(xs, wih, whh, cw, cb):
            T, b, c, L = xs.shape

            def step(h, xr):
                xi = xr.transpose(0, 2, 1).reshape(b * L, c)
                out = _gru_step(xi, h, wih, whh)
                ctx = out.reshape(b, L, c).transpose(0, 2, 1)
                h_new = jnp.tanh(_conv1d(ctx, cw, cb)).transpose(0, 2, 1).reshape(b * L, c)
                return (h_new, ctx)
            h0 = jnp.zeros((b * L, c), xs.dtype)
            _, ctxs = lax.scan(step, h0, xs)
            return ctxs
        b, c, h, w = x.shape
        xs_h = x.transpose(2, 0, 1, 3)
        ctx_above = _direction(xs_h, wih_d, whh_d, cw_d, cb_d).transpose(1, 2, 0, 3)
        ctx_below = _direction(xs_h[::-1], wih_u, whh_u, cw_u, cb_u)[::-1].transpose(1, 2, 0, 3)
        xs_w = x.transpose(3, 0, 1, 2)
        _unused_left = _direction(xs_w, wih_l, whh_l, cw_l, cb_l)
        ctx_left = _direction(xs_w[::-1], wih_r, whh_r, cw_r, cb_r)[::-1].transpose(1, 2, 3, 0)
        ctx_right = jnp.zeros_like(ctx_left)
        context_map = jnp.concatenate([ctx_above, ctx_below, ctx_left, ctx_right], axis=1)
        out = jnp.einsum('bchw,oc->bohw', context_map, w_comb) + b_comb[None, :, None, None]
        return out

    def _gn(v, G=32, eps=1e-05):
        B_, C_, H_, W_ = v.shape
        g = v.reshape(B_, G, C_ // G, H_, W_)
        m = jnp.mean(g, axis=(2, 3, 4), keepdims=True)
        s = jnp.var(g, axis=(2, 3, 4), keepdims=True)
        return ((g - m) / jnp.sqrt(s + eps)).reshape(v.shape)

    def _ln_c(v, eps=1e-06):
        m = jnp.mean(v, axis=1, keepdims=True)
        s = jnp.var(v, axis=1, keepdims=True)
        return (v - m) / jnp.sqrt(s + eps)

    def _ln_t(v, eps=1e-05):
        m = jnp.mean(v, axis=-1, keepdims=True)
        s = jnp.var(v, axis=-1, keepdims=True)
        return (v - m) / jnp.sqrt(s + eps)

    def _to_tokens(v):
        B_, C_, H_, W_ = v.shape
        return v.reshape(B_, C_, H_ * W_).transpose(0, 2, 1)

    def _from_tokens(t, like):
        B_, C_, H_, W_ = like.shape
        return t.transpose(0, 2, 1).reshape(B_, C_, H_, W_)
    x = x + _L0_conv_ref(_gn(x), L0_conv_wih_d, L0_conv_whh_d, L0_conv_cw_d, L0_conv_cb_d, L0_conv_wih_u, L0_conv_whh_u, L0_conv_cw_u, L0_conv_cb_u, L0_conv_wih_l, L0_conv_whh_l, L0_conv_cw_l, L0_conv_cb_l, L0_conv_wih_r, L0_conv_whh_r, L0_conv_cw_r, L0_conv_cb_r, L0_conv_w_comb, L0_conv_b_comb)
    return x

_drawn_inputs = setup_inputs


def setup_inputs(seed=0):
    import zlib

    import numpy as np

    out = dict(_drawn_inputs(seed))
    spreads = {'L0_conv_cb_d': (0.0, 0.1),
     'L0_conv_cb_u': (0.0, 0.272),
     'L0_conv_cb_l': (0.0, 0.1),
     'L0_conv_cb_r': (0.0, 0.1),
     'L0_conv_b_comb': (0.0, 0.1)}
    factors = {}
    for name, (base, spread) in spreads.items():
        noise = np.random.default_rng([zlib.crc32(name.encode()), seed]).standard_normal(out[name].shape)
        drawn = base * np.exp(spread * noise) if base else spread * noise
        out[name] = jnp.asarray(drawn.astype(out[name].dtype))
    for name, factor in factors.items():
        out[name] = (out[name] * factor).astype(out[name].dtype)
    return out
```

```python
import concourse.bass as bass
import concourse.mybir as mybir

B, C, H, W = 8, 128, 32, 32
GROUPS = 32
GROUP_C = C // GROUPS
LINE = W
STEPS = H
COLS = B * LINE
PAD = LINE + 2
SPACE = H * W
DIRS = 3
GATES = 3
TAPS = 3
DIR_BLOCKS = 2 * GATES + TAPS
BLOCKS = DIRS * DIR_BLOCKS + DIRS
SETS = 2 * DIRS + 1
EPS = 1e-5
ACT_SCALE = 512.0
W_TOP = 2.0 ** 14
LEAST_MAX = 2.0 ** -100
HI, LO = 0, 1
OUT_COLS = 512
CHUNK_ROWS = OUT_COLS // W
CHUNKS_B = SPACE // OUT_COLS
RING = 4
HALF_B = B // 2


def build(nc, x_d, w_d, bias_d, out_d):
    from contextlib import ExitStack
    f32, f16, i32 = mybir.dt.float32, mybir.dt.float16, mybir.dt.int32
    ALU, ACT, AX = mybir.AluOpType, mybir.ActivationFunctionType, mybir.AxisListType

    with ExitStack() as ctx:
        def sb(name, shape, dt):
            return ctx.enter_context(nc.sbuf_tensor(name, shape, dt))

        def sem(name):
            return ctx.enter_context(nc.semaphore(name))

        def per_dir(name):
            return [sem(f"{name}_{k}") for k in range(DIRS)]

        ctx_store = [sb(f"ctx_store_{k}", [C, 2, STEPS, B, PAD], f16) for k in range(DIRS)]
        x_rows = sb("x_rows", [C, 2, H, B, W], f16)
        x_cols = sb("x_cols", [C, 2, W, B, H], f16)
        w_parts = sb("w_parts", [C, 2, BLOCKS, C], f16)
        rz = [sb(f"rz_{k}", [C, 2, COLS], f32) for k in range(DIRS)]
        npre = [sb(f"npre_{k}", [C, COLS], f32) for k in range(DIRS)]
        nval = [sb(f"nval_{k}", [C, COLS], f32) for k in range(DIRS)]
        hval = [sb(f"hval_{k}", [C, COLS], f32) for k in range(DIRS)]
        blend = [sb(f"blend_{k}", [C, COLS], f32) for k in range(DIRS)]
        h_parts = [sb(f"h_parts_{k}", [C, 2, COLS], f16) for k in range(DIRS)]
        biases = sb("biases", [C, DIRS + 1], f32)
        absmax = sb("absmax", [C, SETS], f32)
        allmax = sb("allmax", [C, SETS], f32)
        pow2 = sb("pow2", [C, SETS], f32)
        w_scale = sb("w_scale", [C, SETS], f32)
        descale = sb("descale", [C, SETS], f32)
        group_avg = sb("group_avg", [C, C], f32)
        stats = sb("stats", [C, B, CHUNKS_B, 6], f32)
        meanvar = sb("meanvar", [C, B, 2], f32)
        gmean = sb("gmean", [C, B], f32)
        dev = sb("dev", [C, B], f32)
        gvar = sb("gvar", [C, B], f32)
        minus_half = sb("minus_half", [C, B], f32)
        inv_std = sb("inv_std", [C, B], f32)
        x_scale = sb("x_scale", [C, B], f32)
        x32 = ctx_store[0][:].rearrange("p a t b l -> p (a t b l)")[:, 0:2 * B * SPACE] \
            .bitcast(f32).rearrange("p (b h w) -> p b h w", b=B, h=H)
        w32 = ctx_store[1][:].rearrange("p a t b l -> p (a t b l)")[:, 0:2 * BLOCKS * C] \
            .bitcast(f32).rearrange("p (n c) -> p n c", n=BLOCKS)
        x_again = x_rows[:].rearrange("p a h b w -> p (a h b w)").bitcast(f32) \
            .rearrange("p (b s) -> p b s", b=B)

        y_sb = x_cols[:].rearrange("p a w b h -> p (a w b h)").bitcast(f32) \
            .rearrange("p (n s) -> p n s", n=B * CHUNKS_B)

        def bank(name):
            return ctx.enter_context(nc.psum_tensor(name, [C, 512], f32))

        rz_bank = [bank(f"rz_bank_{k}") for k in range(DIRS)]
        n_bank = [bank(f"n_bank_{k}") for k in range(DIRS)]
        conv_bank = [bank(f"conv_bank_{i}") for i in range(2)]
        y_bank = [rz_bank[0], n_bank[0], rz_bank[1], n_bank[1]]

        w_loaded = sem("w_loaded")
        bias_loaded = sem("bias_loaded")
        x_loaded = [sem(f"x_loaded_{b}") for b in range(B)]
        x_reloaded = [sem(f"x_reloaded_{b}") for b in range(B)]
        pool_built = sem("pool_built")
        stats_done = sem("stats_done")
        aggr_done = sem("aggr_done")
        mean_avg = sem("mean_avg")
        dve_chain = sem("dve_chain")
        spread_done = sem("spread_done")
        var_avg = sem("var_avg")
        var_eps = sem("var_eps")
        pow_done = sem("pow_done")
        x_normed = sem("x_normed")
        xrow_hi = sem("xrow_hi")
        xcol_hi = sem("xcol_hi")
        xrow_lo = sem("xrow_lo")
        xcol_lo = sem("xcol_lo")
        max_done = sem("max_done")
        allmax_done = sem("allmax_done")
        scale_done = sem("scale_done")
        w_scaled = sem("w_scaled")
        w_hi_done = sem("w_hi_done")
        w_lo_done = sem("w_lo_done")
        pads_zero = sem("pads_zero")
        rz_ready = per_dir("rz_ready")
        n_ready = per_dir("n_ready")
        conv_ready = per_dir("conv_ready")
        sig_done = per_dir("sig_done")
        rh_done = per_dir("rh_done")
        npre_done = per_dir("npre_done")
        n_done = per_dir("n_done")
        diff_done = per_dir("diff_done")
        zdiff_done = per_dir("zdiff_done")
        ctx_done = per_dir("ctx_done")
        ctx_hi_done = per_dir("ctx_hi_done")
        ctx_lo_done = per_dir("ctx_lo_done")
        h_done = per_dir("h_done")
        h_hi_done = per_dir("h_hi_done")
        h_lo_done = per_dir("h_lo_done")
        y_ready = sem("y_ready")
        y_biased = sem("y_biased")
        y_summed = sem("y_summed")
        y_stored = sem("y_stored")

        def line(k, step):
            return step if k == 0 else step * -1 + (STEPS - 1)

        def lagged(t, j, lag):
            return (j - lag) % DIRS, t + (j - lag) // DIRS

        def exists(step, last=STEPS - 1):
            return not isinstance(step, int) or 0 <= step <= last

        def is_first(step):
            return isinstance(step, int) and step == 0

        def blocks(eng, block):
            for t in (0, 1):
                for j in range(DIRS):
                    block(t, j)
            with eng.Fori(2, STEPS - 1) as t:
                for j in range(DIRS):
                    block(t, j)
            for t in (STEPS - 1, STEPS):
                for j in range(DIRS):
                    block(t, j)

        def w_block(part, k, n):
            return w_parts[:, part, k * DIR_BLOCKS + n, :]

        def gate_scale(k):
            return descale[:, k:k + 1]

        def conv_scale(k):
            return descale[:, DIRS + k:DIRS + k + 1]

        block = ctx.enter_context(nc.Block())

        @block.sync
        def _(sp):
            sp.dma_start(w32, w_d.rearrange("p (n c) -> p n c", n=BLOCKS)).then_inc(w_loaded, 16)
            sp.dma_start(biases[:], bias_d).then_inc(bias_loaded, 16)
            for b in range(B):
                sp.dma_start(x32[:, b, :, :], x_d[b, :, :, :]).then_inc(x_loaded[b], 16)
            sp.wait_ge(n_ready[0], STEPS)
            sp.wait_ge(n_ready[1], STEPS)
            for b in range(B):
                sp.dma_start(x_again[:, b, :], x_d[b, :, :, :].rearrange("c h w -> c (h w)")) \
                    .then_inc(x_reloaded[b], 16)
            for c in range(B * CHUNKS_B):
                b, part = divmod(c, CHUNKS_B)
                sp.wait_ge(y_summed, c + 1)
                sp.dma_start(out_d[b, :, part * CHUNK_ROWS:(part + 1) * CHUNK_ROWS, :]
                             .rearrange("c h w -> c (h w)"), y_sb[:, c, :]) \
                    .then_inc(y_stored, 16)
            sp.wait_ge(y_stored, 16 * B * CHUNKS_B)

        @block.gpsimd
        def _(pool):
            nc.gpsimd.memset(minus_half[:], -0.5)
            nc.gpsimd.memset(group_avg[:], 1.0 / GROUP_C).then_inc(pool_built, 1)
            groups = group_avg[:].rearrange("p (g c) -> p g c", g=GROUPS)
            pool.wait_ge(pool_built, 1)
            nc.gpsimd.affine_select(out=groups, in_=groups, compare_op=ALU.is_ge, fill=0.0, base=0,
                                    pattern=[[-GROUP_C, GROUPS], [0, GROUP_C]],
                                    channel_multiplier=1).then_inc(pool_built, 1)
            pool.wait_ge(pool_built, 2)
            nc.gpsimd.affine_select(out=groups, in_=groups, compare_op=ALU.is_ge, fill=0.0,
                                    base=GROUP_C - 1, pattern=[[GROUP_C, GROUPS], [0, GROUP_C]],
                                    channel_multiplier=-1).then_inc(pool_built, 1)
            ends = ctx_store[2][:, :, :, :, 0:PAD:PAD - 1].rearrange("p a t b e -> p (a t) b e")
            nc.gpsimd.memset(ends, 0.0).then_inc(pads_zero, 1)
            pool.wait_ge(max_done, SETS)
            nc.gpsimd.partition_all_reduce(allmax[:], absmax[:], C, bass.bass_isa.ReduceOp.max) \
                .then_inc(allmax_done, 1)
            done = 0
            for s, (lo, hi) in enumerate(WEIGHT_SETS):
                pool.wait_ge(w_hi_done, s + 1)
                nc.gpsimd.tensor_tensor(out=w_parts[:, LO, lo:hi, :], in0=w32[:, lo:hi, :],
                                        in1=w_parts[:, HI, lo:hi, :], op=ALU.subtract) \
                    .then_inc(w_lo_done, 1)
                if s in (2, 5):
                    half = s // 3
                    pool.wait_ge(var_eps, half + 1)
                    hb = slice(half * HALF_B, (half + 1) * HALF_B)
                    nc.gpsimd.tensor_tensor(out=inv_std[:, hb], in0=gvar[:, hb], in1=minus_half[:, hb],
                                            op=ALU.pow).then_inc(pow_done, 1)
            for b in range(B):
                pool.wait_ge(xrow_lo, b + 1)
                nc.gpsimd.tensor_copy(x_cols[:, LO, :, b, :],
                                      x_rows[:, LO, :, b, :].rearrange("p h w -> p w h")) \
                    .then_inc(xcol_lo, 1)
            pool.wait_ge(w_lo_done, SETS)
            pool.wait_ge(xcol_hi, B)
            for k in (0, 1):
                ends = ctx_store[k][:, :, :, :, 0:PAD:PAD - 1].rearrange("p a t b e -> p (a t) b e")
                nc.gpsimd.memset(ends, 0.0).then_inc(pads_zero, 1)

        @block.scalar
        def _(act):
            act.wait_ge(w_loaded, 16)
            act.wait_ge(scale_done, 1)
            for s, (lo, hi) in enumerate(WEIGHT_SETS):
                nc.scalar.activation(w32[:, lo:hi, :], w32[:, lo:hi, :], ACT.Copy,
                                     scale=w_scale[:, s:s + 1]).then_inc(w_scaled, 1)
            for s, (lo, hi) in enumerate(WEIGHT_SETS):
                act.wait_ge(w_scaled, s + 1)
                nc.scalar.activation(w_parts[:, HI, lo:hi, :], w32[:, lo:hi, :], ACT.Copy) \
                    .then_inc(w_hi_done, 1)
            for b in range(B):
                act.wait_ge(x_normed, b + 1)
                nc.scalar.activation(x_rows[:, HI, :, b, :], x32[:, b, :, :], ACT.Copy) \
                    .then_inc(xrow_hi, 1)
                nc.scalar.activation(x_cols[:, HI, :, b, :],
                                     x32[:, b, :, :].rearrange("p h w -> p w h"), ACT.Copy) \
                    .then_inc(xcol_hi, 1)
            act.wait_ge(bias_loaded, 16)
            act.wait_ge(xrow_lo, B)
            act.wait_ge(pads_zero, DIRS)

            def steps(t, j):
                k, s = lagged(t, j, 2)
                if exists(s, STEPS - 2):
                    act.wait_ge(conv_ready[k], s + 1)
                    nc.scalar.activation(hval[k][:], conv_bank[k % 2][:, 0:COLS], ACT.Tanh,
                                         bias=biases[:, k:k + 1], scale=conv_scale(k)) \
                        .then_inc(h_done[k], 1)
                    act.wait_ge(h_done[k], s + 1)
                    nc.scalar.activation(h_parts[k][:, HI, :], hval[k][:], ACT.Copy, scale=ACT_SCALE) \
                        .then_inc(h_hi_done[k], 1)
                k, s = lagged(t, j, 1)
                if exists(s):
                    act.wait_ge(ctx_done[k], s + 1)
                    nc.scalar.activation(ctx_store[k][:, HI, line(k, s), :, 1:1 + LINE],
                                         blend[k][:].rearrange("p (b l) -> p b l", b=B),
                                         ACT.Copy, scale=ACT_SCALE).then_inc(ctx_hi_done[k], 1)
                k, s = lagged(t, j, 0)
                if exists(s):
                    act.wait_ge(rz_ready[k], s + 1)
                    nc.scalar.activation(rz[k][:].rearrange("p g c -> p (g c)"), rz_bank[k][:],
                                         ACT.Sigmoid, scale=gate_scale(k)).then_inc(sig_done[k], 1)
                    act.wait_ge(npre_done[k], s + 1)
                    nc.scalar.activation(nval[k][:], npre[k][:], ACT.Tanh).then_inc(n_done[k], 1)

            blocks(act, steps)

            for c in range(B * CHUNKS_B):
                act.wait_ge(y_ready, c + 1)
                nc.scalar.activation(y_sb[:, c, :], y_bank[c % RING][:], ACT.Identity,
                                     bias=biases[:, DIRS:DIRS + 1],
                                     scale=descale[:, 2 * DIRS:2 * DIRS + 1]).then_inc(y_biased, 1)

        @block.vector
        def _(dve):
            chained = [0]

            def chain(instruction):
                chained[0] += 1
                instruction.then_inc(dve_chain, 1)
                dve.wait_ge(dve_chain, chained[0])

            dve.wait_ge(w_loaded, 16)
            for s, (lo, hi) in enumerate(WEIGHT_SETS):
                nc.vector.tensor_reduce(out=absmax[:, s:s + 1], in_=w32[:, lo:hi, :].rearrange("p n c -> p (n c)"),
                                        axis=AX.X, op=ALU.max, apply_absolute_value=True).then_inc(max_done, 1)

            def image_stats(b):
                dve.wait_ge(x_loaded[b], 16)
                for i in range(CHUNKS_B):
                    rows = slice(i * CHUNK_ROWS, (i + 1) * CHUNK_ROWS)
                    nc.vector.bn_stats(out=stats[:, b, i, :],
                                       in_=x32[:, b, rows, :].rearrange("p h w -> p (h w)")) \
                        .then_inc(stats_done, 1)
                dve.wait_ge(stats_done, CHUNKS_B * (b + 1))
                nc.vector.bn_aggr(out=meanvar[:, b, :], in_=stats[:, b, :, :].rearrange("p i s -> p (i s)")) \
                    .then_inc(aggr_done, 1)

            def combine(half):
                hb = slice(half * HALF_B, (half + 1) * HALF_B)
                dve.wait_ge(mean_avg, half + 1)
                chain(nc.vector.tensor_copy(gmean[:, hb], conv_bank[0][:, hb]))
                chain(nc.vector.tensor_tensor(out=dev[:, hb], in0=meanvar[:, hb, 0], in1=gmean[:, hb],
                                              op=ALU.subtract))
                chain(nc.vector.tensor_tensor(out=dev[:, hb], in0=dev[:, hb], in1=dev[:, hb], op=ALU.mult))
                nc.vector.tensor_tensor(out=dev[:, hb], in0=dev[:, hb], in1=meanvar[:, hb, 1],
                                        op=ALU.add).then_inc(spread_done, 1)
                dve.wait_ge(var_avg, half + 1)
                nc.vector.tensor_scalar(gvar[:, hb], conv_bank[0][:, B + half * HALF_B:B + (half + 1) * HALF_B],
                                        EPS, None, ALU.add).then_inc(var_eps, 1)
                dve.wait_ge(pow_done, half + 1)
                chain(nc.vector.tensor_scalar(x_scale[:, hb], inv_std[:, hb], ACT_SCALE, None, ALU.mult))

            def normalise(b):
                nc.vector.tensor_scalar(x32[:, b, :, :].rearrange("p h w -> p (h w)"),
                                        x32[:, b, :, :].rearrange("p h w -> p (h w)"),
                                        gmean[:, b:b + 1], x_scale[:, b:b + 1],
                                        ALU.subtract, ALU.mult).then_inc(x_normed, 1)

            def x_lo(b):
                dve.wait_ge(xrow_hi, b + 1)
                nc.vector.tensor_tensor(out=x_rows[:, LO, :, b, :], in0=x32[:, b, :, :],
                                        in1=x_rows[:, HI, :, b, :], op=ALU.subtract).then_inc(xrow_lo, 1)

            image_stats(0)
            dve.wait_ge(allmax_done, 1)
            chain(nc.vector.tensor_scalar(allmax[:], allmax[:], LEAST_MAX, None, ALU.max))
            chain(nc.vector.tensor_scalar(pow2[:].bitcast(i32), allmax[:].bitcast(i32), 0x7F800000, None,
                                          ALU.bitwise_and))
            chain(nc.vector.tensor_scalar(descale[:], pow2[:], 1.0 / (W_TOP * ACT_SCALE), None, ALU.mult))
            chain(nc.vector.reciprocal(w_scale[:], pow2[:]))
            chained[0] += 1
            nc.vector.tensor_scalar(w_scale[:], w_scale[:], W_TOP, None, ALU.mult).then_inc(scale_done, 1)
            chained[0] -= 1
            for b in range(1, HALF_B):
                image_stats(b)
            combine(0)
            for b in range(HALF_B, B):
                image_stats(b)
                normalise(b - HALF_B)
                if b > HALF_B:
                    x_lo(b - HALF_B - 1)
            combine(1)
            for b in range(HALF_B, B):
                normalise(b)
                x_lo(b - 1)
            x_lo(B - 1)

            def steps(t, j):
                k, s = lagged(t, j, 1)
                if exists(s):
                    z = rz[k][:, 1, :]
                    if is_first(s):
                        dve.wait_ge(n_done[k], 1)
                        nc.vector.scalar_tensor_tensor(blend[k][:], nval[k][:], -1.0, z, ALU.mult,
                                                       ALU.mult).then_inc(zdiff_done[k], 1)
                    else:
                        dve.wait_ge(diff_done[k], s)
                        nc.vector.tensor_tensor(out=blend[k][:], in0=z, in1=blend[k][:],
                                                op=ALU.mult).then_inc(zdiff_done[k], 1)
                    dve.wait_ge(zdiff_done[k], s + 1)
                    nc.vector.tensor_tensor(out=blend[k][:], in0=blend[k][:], in1=nval[k][:],
                                            op=ALU.add).then_inc(ctx_done[k], 1)
                k2, s2 = lagged(t, j, 2)
                if exists(s2, STEPS - 2):
                    dve.wait_ge(h_hi_done[k2], s2 + 1)
                    nc.vector.scalar_tensor_tensor(h_parts[k2][:, LO, :], hval[k2][:], ACT_SCALE,
                                                   h_parts[k2][:, HI, :], ALU.mult,
                                                   ALU.subtract).then_inc(h_lo_done[k2], 1)
                if exists(s):
                    dve.wait_ge(ctx_hi_done[k], s + 1)
                    nc.vector.scalar_tensor_tensor(
                        ctx_store[k][:, LO, line(k, s), :, 1:1 + LINE],
                        blend[k][:].rearrange("p (b l) -> p b l", b=B), ACT_SCALE,
                        ctx_store[k][:, HI, line(k, s), :, 1:1 + LINE], ALU.mult,
                        ALU.subtract).then_inc(ctx_lo_done[k], 1)
                k, s = lagged(t, j, 0)
                if exists(s):
                    dve.wait_ge(n_ready[k], s + 1)
                    if is_first(s):
                        nc.vector.tensor_scalar(npre[k][:], n_bank[k][:, 0:COLS], gate_scale(k), None,
                                                ALU.mult).then_inc(npre_done[k], 1)
                    else:
                        dve.wait_ge(sig_done[k], s + 1)
                        nc.vector.scalar_tensor_tensor(npre[k][:], n_bank[k][:, COLS:2 * COLS],
                                                       gate_scale(k), rz[k][:, 0, :], ALU.mult,
                                                       ALU.mult).then_inc(rh_done[k], 1)
                        dve.wait_ge(rh_done[k], s)
                        nc.vector.scalar_tensor_tensor(npre[k][:], n_bank[k][:, 0:COLS], gate_scale(k),
                                                       npre[k][:], ALU.mult,
                                                       ALU.add).then_inc(npre_done[k], 1)
                        dve.wait_ge(n_done[k], s + 1)
                        nc.vector.tensor_tensor(out=blend[k][:], in0=hval[k][:], in1=nval[k][:],
                                                op=ALU.subtract).then_inc(diff_done[k], 1)

            blocks(dve, steps)

            for c in range(B * CHUNKS_B):
                b, part = divmod(c, CHUNKS_B)
                dve.wait_ge(y_biased, c + 1)
                if part == 0:
                    dve.wait_ge(x_reloaded[b], 16)
                nc.vector.tensor_tensor(out=y_sb[:, c, :], in0=y_sb[:, c, :],
                                        in1=x_again[:, b, part * OUT_COLS:(part + 1) * OUT_COLS],
                                        op=ALU.add).then_inc(y_summed, 1)

        @block.tensor
        def _(pe):
            pe.wait_ge(pool_built, 3)
            for half in range(2):
                hb = slice(half * HALF_B, (half + 1) * HALF_B)
                pe.wait_ge(aggr_done, (half + 1) * HALF_B)
                nc.tensor.matmul(conv_bank[0][:, hb], group_avg[:], meanvar[:, hb, 0], start=True,
                                 stop=True).then_inc(mean_avg, 1)
                pe.wait_ge(spread_done, half + 1)
                nc.tensor.matmul(conv_bank[0][:, B + half * HALF_B:B + (half + 1) * HALF_B], group_avg[:],
                                 dev[:, hb], start=True, stop=True).then_inc(var_avg, 1)

            def passes(out, k, n, parts, hi_or_lo, start=False, stop=False):
                last = nc.tensor.matmul(out, w_block(HI, k, n), parts(hi_or_lo), start=start,
                                        stop=stop and hi_or_lo == LO, skip_group_check=True)
                if hi_or_lo == HI:
                    last = nc.tensor.matmul(out, w_block(LO, k, n), parts(HI), start=False, stop=False,
                                            skip_group_check=True)
                return last

            def input_products(k, s):
                first = is_first(s)
                store = x_cols if k == 2 else x_rows

                def x_parts(part):
                    return store[:, part, line(k, s), :, :].rearrange("p b l -> p (b l)")

                if not first:
                    pe.wait_ge(sig_done[k], s)
                for gate in range(2):
                    out = rz_bank[k][:, gate * COLS:(gate + 1) * COLS]
                    passes(out, k, gate, x_parts, HI, start=gate == 0)
                    last = passes(out, k, gate, x_parts, LO, stop=first and gate == 1)
                if first:
                    last.then_inc(rz_ready[k], 1)
                else:
                    pe.wait_ge(npre_done[k], s)
                passes(n_bank[k][:, 0:COLS], k, 2, x_parts, HI, start=True)
                last = passes(n_bank[k][:, 0:COLS], k, 2, x_parts, LO, stop=first)
                if first:
                    last.then_inc(n_ready[k], 1)

            def hidden_products(k, s):
                def parts(part):
                    return h_parts[k][:, part, :]

                pe.wait_ge(h_hi_done[k], s)
                for gate in range(2):
                    passes(rz_bank[k][:, gate * COLS:(gate + 1) * COLS], k, GATES + gate, parts, HI)
                pe.wait_ge(h_lo_done[k], s)
                for gate in range(2):
                    last = passes(rz_bank[k][:, gate * COLS:(gate + 1) * COLS], k, GATES + gate, parts, LO,
                                  stop=gate == 1)
                last.then_inc(rz_ready[k], 1)
                passes(n_bank[k][:, COLS:2 * COLS], k, GATES + 2, parts, HI)
                passes(n_bank[k][:, COLS:2 * COLS], k, GATES + 2, parts, LO, stop=True) \
                    .then_inc(n_ready[k], 1)

            def convolution(k, s):
                out = conv_bank[k % 2][:, 0:COLS].rearrange("p (b l) -> p b l", b=B)
                if k == 2:
                    pe.wait_ge(h_done[0], s + 1)
                elif not is_first(s):
                    pe.wait_ge(h_done[1 if k == 1 else 2], s)
                pe.wait_ge(ctx_hi_done[k], s + 1)
                for part in (HI, LO):
                    if part == LO:
                        pe.wait_ge(ctx_lo_done[k], s + 1)
                    for tap in range(TAPS):
                        last = passes(out, k, 2 * GATES + tap,
                                      lambda p: ctx_store[k][:, p, line(k, s), :, tap:tap + LINE],
                                      part, start=part == HI and tap == 0, stop=tap == TAPS - 1)
                last.then_inc(conv_ready[k], 1)

            def steps(t, j):
                k, s = lagged(t, j, 0)
                if exists(s) and not is_first(s):
                    hidden_products(k, s)
                k, s = lagged(t, j, -1)
                if exists(s):
                    input_products(k, s)
                k, s = lagged(t, j, 1)
                if exists(s, STEPS - 2):
                    convolution(k, s)

            pe.wait_ge(w_lo_done, SETS)
            pe.wait_ge(xrow_lo, B)
            pe.wait_ge(xcol_lo, B)
            pe.wait_ge(xcol_hi, B)
            pe.wait_ge(var_eps, 2)
            input_products(0, 0)
            blocks(pe, steps)

            def chunk_part(c, k, start, stop):
                b, part = divmod(c, CHUNKS_B)
                rows = slice(part * CHUNK_ROWS, (part + 1) * CHUNK_ROWS)
                out = y_bank[c % RING][:].rearrange("p (h w) -> p h w", h=CHUNK_ROWS)

                def ctx_part(p):
                    if k == 2:
                        cells = slice(1 + part * CHUNK_ROWS, 1 + (part + 1) * CHUNK_ROWS)
                        return ctx_store[2][:, p, :, b, cells].rearrange("p w h -> p h w")
                    return ctx_store[k][:, p, rows, b, 1:1 + LINE]

                wk = DIRS * DIR_BLOCKS + k
                nc.tensor.matmul(out, w_parts[:, HI, wk, :], ctx_part(HI), start=start, stop=False,
                                 skip_group_check=True)
                nc.tensor.matmul(out, w_parts[:, LO, wk, :], ctx_part(HI), start=False, stop=False,
                                 skip_group_check=True)
                return nc.tensor.matmul(out, w_parts[:, HI, wk, :], ctx_part(LO), start=False, stop=stop,
                                        skip_group_check=True)

            for k in range(DIRS - 1):
                pe.wait_ge(ctx_lo_done[k], STEPS)
            for c0 in range(0, B * CHUNKS_B, RING):
                for c in range(c0, c0 + RING):
                    if c >= RING:
                        pe.wait_ge(y_biased, c - RING + 1)
                    chunk_part(c, 0, True, False)
                    chunk_part(c, 1, False, False)
                if c0 == 0:
                    pe.wait_ge(ctx_lo_done[2], STEPS)
                for c in range(c0, c0 + RING):
                    chunk_part(c, 2, False, True).then_inc(y_ready, 1)


def _weight_sets():
    gates = [(k * DIR_BLOCKS, k * DIR_BLOCKS + 2 * GATES) for k in range(DIRS)]
    convs = [(k * DIR_BLOCKS + 2 * GATES, (k + 1) * DIR_BLOCKS) for k in range(DIRS)]
    return gates + convs + [(DIRS * DIR_BLOCKS, BLOCKS)]


WEIGHT_SETS = _weight_sets()


def kernel(**inputs):
    import numpy as np
    import concourse.bacc as bacc
    from concourse.bass_utils import run_bass_kernel_spmd

    blocks = []
    for d in ("d", "u", "r"):
        blocks.append(np.asarray(inputs[f"L0_conv_wih_{d}"]).T)
        blocks.append(np.asarray(inputs[f"L0_conv_whh_{d}"]).T)
        blocks.append(np.asarray(inputs[f"L0_conv_cw_{d}"]).transpose(1, 2, 0).reshape(C, TAPS * C))
    blocks.append(np.asarray(inputs["L0_conv_w_comb"]).T.reshape(DIRS + 1, C, C)[:DIRS]
                  .transpose(1, 0, 2).reshape(C, DIRS * C))
    arrays = {
        "x": np.ascontiguousarray(inputs["x"]),
        "weights": np.ascontiguousarray(np.concatenate(blocks, axis=1)),
        "biases": np.ascontiguousarray(np.stack(
            [np.asarray(inputs[n]) for n in ("L0_conv_cb_d", "L0_conv_cb_u", "L0_conv_cb_r", "L0_conv_b_comb")],
            axis=1)),
    }
    nc = bacc.Bacc("TRN2", target_bir_lowering=False, num_devices=1)
    aps = [nc.dram_tensor(f"{n}_dram", a.shape, mybir.dt.from_np(a.dtype), kind="ExternalInput").ap()
           for n, a in arrays.items()]
    out = nc.dram_tensor("out_dram", (B, C, H, W), mybir.dt.float32, kind="ExternalOutput").ap()
    build(nc, *aps, out)
    return run_bass_kernel_spmd(nc, [{f"{n}_dram": a for n, a in arrays.items()}], core_ids=[0]).results[0]["out_dram"]
```

```python
import concourse.bass as bass
import concourse.mybir as mybir

B, C, H, W = 8, 128, 32, 32
GROUPS = 32
GROUP_C = C // GROUPS
LINE = W
STEPS = H
COLS = B * LINE
PAD = LINE + 2
SPACE = H * W
DIRS = 3
GATES = 3
TAPS = 3
DIR_BLOCKS = 2 * GATES + TAPS
BLOCKS = DIRS * DIR_BLOCKS + DIRS
SETS = 2 * DIRS + 1
EPS = 1e-5
ACT_SCALE = 512.0
W_TOP = 2.0 ** 14
LEAST_MAX = 2.0 ** -100
HI, LO = 0, 1
OUT_COLS = 512
CHUNK_ROWS = OUT_COLS // W
CHUNKS_B = SPACE // OUT_COLS
RING = 4
HALF_B = B // 2


def build(nc, x_d, w_d, bias_d, out_d):
    from contextlib import ExitStack
    f32, f16, i32 = mybir.dt.float32, mybir.dt.float16, mybir.dt.int32
    ALU, ACT, AX = mybir.AluOpType, mybir.ActivationFunctionType, mybir.AxisListType

    with ExitStack() as ctx:
        def sb(name, shape, dt):
            return ctx.enter_context(nc.sbuf_tensor(name, shape, dt))

        def sem(name):
            return ctx.enter_context(nc.semaphore(name))

        def per_dir(name):
            return [sem(f"{name}_{k}") for k in range(DIRS)]

        ctx_store = [sb(f"ctx_store_{k}", [C, 2, STEPS, B, PAD], f16) for k in range(DIRS)]
        x_rows = sb("x_rows", [C, 2, H, B, W], f16)
        x_col = sb("x_col", [C, 2, B, H], f16)
        x32 = sb("x32", [C, B, H, W], f32)
        w_parts = sb("w_parts", [C, 2, BLOCKS, C], f16)
        rz = [sb(f"rz_{k}", [C, 2, COLS], f32) for k in range(DIRS)]
        npre = [sb(f"npre_{k}", [C, COLS], f32) for k in range(DIRS)]
        nval = [sb(f"nval_{k}", [C, COLS], f32) for k in range(DIRS)]
        hval = [sb(f"hval_{k}", [C, COLS], f32) for k in range(DIRS)]
        context = [sb(f"context_{k}", [C, B, PAD], f32) for k in range(DIRS)]
        h_parts = [sb(f"h_parts_{k}", [C, 2, COLS], f16) for k in range(DIRS)]
        biases = sb("biases", [C, DIRS + 1], f32)
        absmax = sb("absmax", [C, SETS], f32)
        allmax = sb("allmax", [C, SETS], f32)
        pow2 = sb("pow2", [C, SETS], f32)
        w_scale = sb("w_scale", [C, SETS], f32)
        descale = sb("descale", [C, SETS], f32)
        group_avg = sb("group_avg", [C, C], f32)
        stats = sb("stats", [C, B, CHUNKS_B, 6], f32)
        meanvar = sb("meanvar", [C, B, 2], f32)
        gmean = sb("gmean", [C, B], f32)
        dev = sb("dev", [C, B], f32)
        gvar = sb("gvar", [C, B], f32)
        minus_half = sb("minus_half", [C, B], f32)
        inv_std = sb("inv_std", [C, B], f32)
        x_scale = sb("x_scale", [C, B], f32)
        x_norm = ctx_store[0][:].rearrange("p a t b l -> p (a t b l)")[:, 0:2 * B * SPACE] \
            .bitcast(f32).rearrange("p (b h w) -> p b h w", b=B, h=H)
        w32 = ctx_store[1][:].rearrange("p a t b l -> p (a t b l)")[:, 0:2 * BLOCKS * C] \
            .bitcast(f32).rearrange("p (n c) -> p n c", n=BLOCKS)
        y_sb = x_rows[:].rearrange("p a h b w -> p (a h b w)").bitcast(f32) \
            .rearrange("p (n s) -> p n s", n=B * CHUNKS_B)

        def bank(name):
            return ctx.enter_context(nc.psum_tensor(name, [C, 512], f32))

        rz_bank = [bank(f"rz_bank_{k}") for k in range(DIRS)]
        n_bank = [bank(f"n_bank_{k}") for k in range(DIRS)]
        conv_bank = [bank(f"conv_bank_{i}") for i in range(2)]
        y_bank = [rz_bank[0], n_bank[0], rz_bank[1], n_bank[1]]

        w_loaded = per_dir("w_loaded")
        bias_loaded = sem("bias_loaded")
        x_loaded = [sem(f"x_loaded_{b}") for b in range(B)]
        pool_built = sem("pool_built")
        sides_zero = sem("sides_zero")
        stats_done = sem("stats_done")
        aggr_done = sem("aggr_done")
        mean_avg = sem("mean_avg")
        dve_chain = sem("dve_chain")
        spread_done = sem("spread_done")
        var_avg = sem("var_avg")
        var_eps = sem("var_eps")
        pow_done = sem("pow_done")
        x_normed = sem("x_normed")
        x_hi_done = sem("x_hi_done")
        x_lo_pool = sem("x_lo_pool")
        x_lo_dve = sem("x_lo_dve")
        x_col_done = sem("x_col_done")
        max_done = sem("max_done")
        allmax_done = sem("allmax_done")
        scale_done = sem("scale_done")
        w_scaled = sem("w_scaled")
        w_hi_done = sem("w_hi_done")
        w_lo_done = sem("w_lo_done")
        rz_ready = per_dir("rz_ready")
        n_ready = per_dir("n_ready")
        conv_ready = per_dir("conv_ready")
        sig_done = per_dir("sig_done")
        rh_done = per_dir("rh_done")
        npre_done = per_dir("npre_done")
        n_done = per_dir("n_done")
        zn_done = per_dir("zn_done")
        ctx_done = per_dir("ctx_done")
        ctx_hi_done = per_dir("ctx_hi_done")
        ctx_lo_done = per_dir("ctx_lo_done")
        h_done = per_dir("h_done")
        h_hi_done = per_dir("h_hi_done")
        h_lo_done = per_dir("h_lo_done")
        y_ready = sem("y_ready")
        y_biased = sem("y_biased")
        y_summed = sem("y_summed")
        y_stored = sem("y_stored")

        def line(k, step):
            return step if k == 0 else step * -1 + (STEPS - 1)

        def lagged(t, j, lag):
            return (j - lag) % DIRS, t + (j - lag) // DIRS

        def exists(step, last=STEPS - 1):
            return not isinstance(step, int) or 0 <= step <= last

        def is_first(step):
            return isinstance(step, int) and step == 0

        def blocks(eng, block):
            for t in (0, 1):
                for j in range(DIRS):
                    block(t, j)
            with eng.Fori(2, STEPS - 1) as t:
                for j in range(DIRS):
                    block(t, j)
            for t in (STEPS - 1, STEPS):
                for j in range(DIRS):
                    block(t, j)

        def ahead(eng, *operands):
            for x in operands:
                if isinstance(x, int):
                    continue
                if isinstance(x, bass.AP):
                    eng.lower_ap(x)
                else:
                    eng.compute_val(x)

        def context_lines(k, s, part):
            return ctx_store[k][:, part, line(k, s), :, :].rearrange("p b l -> p (b l)")

        def w_block(part, k, n):
            return w_parts[:, part, k * DIR_BLOCKS + n, :]

        def gate_scale(k):
            return descale[:, k:k + 1]

        def conv_scale(k):
            return descale[:, DIRS + k:DIRS + k + 1]

        block = ctx.enter_context(nc.Block())

        @block.sync
        def _(sp):
            for b in range(B):
                if b < DIRS:
                    lo, hi = b * DIR_BLOCKS, (b + 1) * DIR_BLOCKS if b < DIRS - 1 else BLOCKS
                    sp.dma_start(w32[:, lo:hi, :], w_d[:, lo * C:hi * C].rearrange("p (n c) -> p n c", c=C)) \
                        .then_inc(w_loaded[b], 16)
                sp.dma_start(x32[:, b, :, :], x_d[b, :, :, :]).then_inc(x_loaded[b], 16)
            sp.dma_start(biases[:], bias_d).then_inc(bias_loaded, 16)
            for c in range(B * CHUNKS_B):
                b, part = divmod(c, CHUNKS_B)
                sp.wait_ge(y_summed, c + 1)
                sp.dma_start(out_d[b, :, part * CHUNK_ROWS:(part + 1) * CHUNK_ROWS, :]
                             .rearrange("c h w -> c (h w)"), y_sb[:, c, :]) \
                    .then_inc(y_stored, 16)
            sp.wait_ge(y_stored, 16 * B * CHUNKS_B)

        @block.gpsimd
        def _(pool):
            nc.gpsimd.memset(minus_half[:], -0.5)
            nc.gpsimd.memset(group_avg[:], 1.0 / GROUP_C).then_inc(pool_built, 1)
            groups = group_avg[:].rearrange("p (g c) -> p g c", g=GROUPS)
            pool.wait_ge(pool_built, 1)
            nc.gpsimd.affine_select(out=groups, in_=groups, compare_op=ALU.is_ge, fill=0.0, base=0,
                                    pattern=[[-GROUP_C, GROUPS], [0, GROUP_C]],
                                    channel_multiplier=1).then_inc(pool_built, 1)
            pool.wait_ge(pool_built, 2)
            nc.gpsimd.affine_select(out=groups, in_=groups, compare_op=ALU.is_ge, fill=0.0,
                                    base=GROUP_C - 1, pattern=[[GROUP_C, GROUPS], [0, GROUP_C]],
                                    channel_multiplier=-1).then_inc(pool_built, 1)
            for k in range(DIRS):
                nc.gpsimd.memset(context[k][:, :, 0:PAD:PAD - 1], 0.0).then_inc(sides_zero, 1)
            pool.wait_ge(max_done, SETS)
            nc.gpsimd.partition_all_reduce(allmax[:], absmax[:], C, bass.bass_isa.ReduceOp.max) \
                .then_inc(allmax_done, 1)
            for s, (_, lo, hi) in enumerate(WEIGHT_SETS):
                if s in POW_BEFORE:
                    half = POW_BEFORE.index(s)
                    pool.wait_ge(var_eps, half + 1)
                    hb = slice(half * HALF_B, (half + 1) * HALF_B)
                    nc.gpsimd.tensor_tensor(out=inv_std[:, hb], in0=gvar[:, hb], in1=minus_half[:, hb],
                                            op=ALU.pow).then_inc(pow_done, 1)
                pool.wait_ge(w_hi_done, s + 1)
                nc.gpsimd.tensor_tensor(out=w_parts[:, LO, lo:hi, :], in0=w32[:, lo:hi, :],
                                        in1=w_parts[:, HI, lo:hi, :], op=ALU.subtract) \
                    .then_inc(w_lo_done, 1)
            for b in range(POOL_IMAGES):
                pool.wait_ge(x_hi_done, b + 1)
                nc.gpsimd.tensor_tensor(out=x_rows[:, LO, :, b, :], in0=x_norm[:, b, :, :],
                                        in1=x_rows[:, HI, :, b, :], op=ALU.subtract).then_inc(x_lo_pool, 1)

        @block.scalar
        def _(act):
            act.wait_ge(scale_done, 1)

            def scale_weights(s):
                n, lo, hi = WEIGHT_SETS[s]
                nc.scalar.activation(w32[:, lo:hi, :], w32[:, lo:hi, :], ACT.Copy,
                                     scale=w_scale[:, n:n + 1]).then_inc(w_scaled, 1)

            scale_weights(0)
            for s, (_, lo, hi) in enumerate(WEIGHT_SETS):
                if s + 1 < SETS:
                    scale_weights(s + 1)
                act.wait_ge(w_scaled, s + 1)
                nc.scalar.activation(w_parts[:, HI, lo:hi, :], w32[:, lo:hi, :], ACT.Copy) \
                    .then_inc(w_hi_done, 1)
            for b in range(B):
                act.wait_ge(x_normed, b + 1)
                nc.scalar.activation(x_rows[:, HI, :, b, :], x_norm[:, b, :, :], ACT.Copy) \
                    .then_inc(x_hi_done, 1)
            act.wait_ge(bias_loaded, 16)
            act.wait_ge(x_lo_pool, POOL_IMAGES)
            act.wait_ge(x_lo_dve, B - POOL_IMAGES)
            act.wait_ge(sides_zero, DIRS)

            def column(s):
                nc.scalar.activation(x_col[:], x_rows[:, :, :, :, line(2, s)].rearrange("p a h b -> p a b h"),
                                     ACT.Copy).then_inc(x_col_done, 1)

            def gates(k, s):
                act.wait_ge(rz_ready[k], s + 1)
                nc.scalar.activation(rz[k][:].rearrange("p g c -> p (g c)"), rz_bank[k][:],
                                     ACT.Sigmoid, scale=gate_scale(k)).then_inc(sig_done[k], 1)

            def steps(t, j):
                k, s = lagged(t, j, 0)
                if exists(s):
                    ahead(act, s + 1, line(k, s) * (B * PAD))
                    act.wait_ge(npre_done[k], s + 1)
                    nc.scalar.activation(nval[k][:], npre[k][:], ACT.Tanh).then_inc(n_done[k], 1)
                k, s = lagged(t, j, 1)
                if exists(s, STEPS - 2):
                    act.wait_ge(conv_ready[k], s + 1)
                    nc.scalar.activation(hval[k][:], conv_bank[k % 2][:, 0:COLS], ACT.Tanh,
                                         bias=biases[:, k:k + 1], scale=conv_scale(k)) \
                        .then_inc(h_done[k], 1)
                k, s = lagged(t, j, -1)
                if exists(s):
                    gates(k, s)
                k, s = lagged(t, j, 0)
                if exists(s):
                    act.wait_ge(ctx_done[k], s + 1)
                    nc.scalar.activation(context_lines(k, s, HI),
                                         context[k][:].rearrange("p b l -> p (b l)"),
                                         ACT.Copy, scale=ACT_SCALE).then_inc(ctx_hi_done[k], 1)
                k, s = lagged(t, j, 1)
                if exists(s, STEPS - 2):
                    act.wait_ge(h_done[k], s + 1)
                    nc.scalar.activation(h_parts[k][:, HI, :], hval[k][:], ACT.Copy, scale=ACT_SCALE) \
                        .then_inc(h_hi_done[k], 1)
                if j == DIRS - 1 and exists(t + 1):
                    column(t + 1)

            column(0)
            gates(0, 0)
            blocks(act, steps)

            for c in range(B * CHUNKS_B):
                act.wait_ge(y_ready, c + 1)
                nc.scalar.activation(y_sb[:, c, :], y_bank[c % RING][:], ACT.Identity,
                                     bias=biases[:, DIRS:DIRS + 1],
                                     scale=descale[:, 2 * DIRS:2 * DIRS + 1]).then_inc(y_biased, 1)

        @block.vector
        def _(dve):
            chained = [0]

            def chain(instruction):
                chained[0] += 1
                instruction.then_inc(dve_chain, 1)
                dve.wait_ge(dve_chain, chained[0])

            def weight_max(k):
                dve.wait_ge(w_loaded[k], 16)
                for n, lo, hi in WEIGHT_SETS[2 * k:2 * k + 2 if k < DIRS - 1 else SETS]:
                    nc.vector.tensor_reduce(out=absmax[:, n:n + 1],
                                            in_=w32[:, lo:hi, :].rearrange("p n c -> p (n c)"), axis=AX.X,
                                            op=ALU.max, apply_absolute_value=True).then_inc(max_done, 1)

            def image_stats(b):
                dve.wait_ge(x_loaded[b], 16)
                for i in range(CHUNKS_B):
                    rows = slice(i * CHUNK_ROWS, (i + 1) * CHUNK_ROWS)
                    nc.vector.bn_stats(out=stats[:, b, i, :],
                                       in_=x32[:, b, rows, :].rearrange("p h w -> p (h w)")) \
                        .then_inc(stats_done, 1)
                dve.wait_ge(stats_done, CHUNKS_B * (b + 1))
                nc.vector.bn_aggr(out=meanvar[:, b, :], in_=stats[:, b, :, :].rearrange("p i s -> p (i s)")) \
                    .then_inc(aggr_done, 1)

            def combine(half):
                hb = slice(half * HALF_B, (half + 1) * HALF_B)
                dve.wait_ge(mean_avg, half + 1)
                chain(nc.vector.tensor_copy(gmean[:, hb], conv_bank[0][:, hb]))
                chain(nc.vector.tensor_tensor(out=dev[:, hb], in0=meanvar[:, hb, 0], in1=gmean[:, hb],
                                              op=ALU.subtract))
                chain(nc.vector.tensor_tensor(out=dev[:, hb], in0=dev[:, hb], in1=dev[:, hb], op=ALU.mult))
                nc.vector.tensor_tensor(out=dev[:, hb], in0=dev[:, hb], in1=meanvar[:, hb, 1],
                                        op=ALU.add).then_inc(spread_done, 1)
                dve.wait_ge(var_avg, half + 1)
                nc.vector.tensor_scalar(gvar[:, hb], conv_bank[0][:, B + half * HALF_B:B + (half + 1) * HALF_B],
                                        EPS, None, ALU.add).then_inc(var_eps, 1)

            def scales(half):
                hb = slice(half * HALF_B, (half + 1) * HALF_B)
                dve.wait_ge(pow_done, half + 1)
                chain(nc.vector.tensor_scalar(x_scale[:, hb], inv_std[:, hb], ACT_SCALE, None, ALU.mult))

            def normalise(b):
                nc.vector.tensor_scalar(x_norm[:, b, :, :].rearrange("p h w -> p (h w)"),
                                        x32[:, b, :, :].rearrange("p h w -> p (h w)"),
                                        gmean[:, b:b + 1], x_scale[:, b:b + 1],
                                        ALU.subtract, ALU.mult).then_inc(x_normed, 1)

            def x_lo(b):
                dve.wait_ge(x_hi_done, b + 1)
                nc.vector.tensor_tensor(out=x_rows[:, LO, :, b, :], in0=x_norm[:, b, :, :],
                                        in1=x_rows[:, HI, :, b, :], op=ALU.subtract).then_inc(x_lo_dve, 1)

            for b in range(DIRS):
                weight_max(b)
                image_stats(b)
            dve.wait_ge(allmax_done, 1)
            chain(nc.vector.tensor_scalar(allmax[:], allmax[:], LEAST_MAX, None, ALU.max))
            chain(nc.vector.tensor_scalar(pow2[:].bitcast(i32), allmax[:].bitcast(i32), 0x7F800000, None,
                                          ALU.bitwise_and))
            chain(nc.vector.tensor_scalar(descale[:], pow2[:], 1.0 / (W_TOP * ACT_SCALE), None, ALU.mult))
            chain(nc.vector.reciprocal(w_scale[:], pow2[:]))
            chained[0] += 1
            nc.vector.tensor_scalar(w_scale[:], w_scale[:], W_TOP, None, ALU.mult).then_inc(scale_done, 1)
            chained[0] -= 1
            for b in range(DIRS, HALF_B):
                image_stats(b)
            combine(0)
            image_stats(HALF_B)
            scales(0)
            for b in range(HALF_B + 1, B):
                normalise(b - HALF_B - 1)
                image_stats(b)
            combine(1)
            normalise(HALF_B - 1)
            scales(1)
            for b in range(HALF_B, B):
                normalise(b)
            for b in range(POOL_IMAGES, B):
                x_lo(b)

            def lines(ap):
                return ap.rearrange("p (b l) -> p b l", b=B)

            def blend(k, s):
                zh, z = rz[k][:, 0, :], rz[k][:, 1, :]
                dve.wait_ge(n_done[k], s + 1)
                if is_first(s):
                    dve.wait_ge(sig_done[k], 1)
                nc.vector.scalar_tensor_tensor(nval[k][:], z, 1.0, nval[k][:], ALU.subtract,
                                               ALU.mult).then_inc(zn_done[k], 1)
                dve.wait_ge(zn_done[k], s + 1)
                if is_first(s):
                    nc.vector.tensor_scalar(context[k][:, :, 1:1 + LINE], lines(nval[k][:]), -1.0, None,
                                            ALU.mult).then_inc(ctx_done[k], 1)
                else:
                    nc.vector.tensor_tensor(out=context[k][:, :, 1:1 + LINE], in0=lines(zh),
                                            in1=lines(nval[k][:]), op=ALU.subtract).then_inc(ctx_done[k], 1)

            def reset_hidden(k, s):
                dve.wait_ge(sig_done[k], s + 1)
                dve.wait_ge(n_ready[k], s + 1)
                nc.vector.scalar_tensor_tensor(npre[k][:], n_bank[k][:, COLS:2 * COLS], gate_scale(k),
                                               rz[k][:, 0, :], ALU.mult, ALU.mult).then_inc(rh_done[k], 1)

            def context_lo(k, s):
                dve.wait_ge(ctx_hi_done[k], s + 1)
                nc.vector.scalar_tensor_tensor(
                    context_lines(k, s, LO), context[k][:].rearrange("p b l -> p (b l)"), ACT_SCALE,
                    context_lines(k, s, HI), ALU.mult, ALU.subtract).then_inc(ctx_lo_done[k], 1)

            def tanh_argument(k, s):
                if is_first(s):
                    dve.wait_ge(n_ready[k], 1)
                    nc.vector.tensor_scalar(npre[k][:], n_bank[k][:, 0:COLS], gate_scale(k), None,
                                            ALU.mult).then_inc(npre_done[k], 1)
                else:
                    dve.wait_ge(rh_done[k], s)
                    nc.vector.scalar_tensor_tensor(npre[k][:], n_bank[k][:, 0:COLS], gate_scale(k),
                                                   npre[k][:], ALU.mult, ALU.add).then_inc(npre_done[k], 1)

            def hidden_lo(k, s):
                dve.wait_ge(h_hi_done[k], s + 1)
                nc.vector.scalar_tensor_tensor(h_parts[k][:, LO, :], hval[k][:], ACT_SCALE,
                                               h_parts[k][:, HI, :], ALU.mult,
                                               ALU.subtract).then_inc(h_lo_done[k], 1)

            def z_times_h(k):
                nc.vector.tensor_tensor(out=rz[k][:, 0, :], in0=rz[k][:, 1, :], in1=hval[k][:], op=ALU.mult)

            def steps(t, j):
                now, nxt, before = lagged(t, j, 0), lagged(t, j, -1), lagged(t, j, 1)
                if exists(now[1]):
                    ahead(dve, now[1] + 1, context_lines(*now, HI), context_lines(*now, LO))
                    blend(*now)
                if exists(nxt[1]) and not is_first(nxt[1]):
                    reset_hidden(*nxt)
                if exists(now[1]):
                    context_lo(*now)
                if exists(nxt[1]):
                    tanh_argument(*nxt)
                if exists(before[1], STEPS - 2):
                    hidden_lo(*before)
                if exists(nxt[1]) and not is_first(nxt[1]):
                    z_times_h(nxt[0])

            dve.wait_ge(sides_zero, DIRS)
            tanh_argument(0, 0)
            blocks(dve, steps)

            for c in range(B * CHUNKS_B):
                b, part = divmod(c, CHUNKS_B)
                dve.wait_ge(y_biased, c + 1)
                nc.vector.tensor_tensor(out=y_sb[:, c, :], in0=y_sb[:, c, :],
                                        in1=x32[:, b, part * CHUNK_ROWS:(part + 1) * CHUNK_ROWS, :]
                                        .rearrange("p h w -> p (h w)"),
                                        op=ALU.add).then_inc(y_summed, 1)

        @block.tensor
        def _(pe):
            pe.wait_ge(pool_built, 3)
            for half in range(2):
                hb = slice(half * HALF_B, (half + 1) * HALF_B)
                pe.wait_ge(aggr_done, (half + 1) * HALF_B)
                nc.tensor.matmul(conv_bank[0][:, hb], group_avg[:], meanvar[:, hb, 0], start=True,
                                 stop=True).then_inc(mean_avg, 1)
                pe.wait_ge(spread_done, half + 1)
                nc.tensor.matmul(conv_bank[0][:, B + half * HALF_B:B + (half + 1) * HALF_B], group_avg[:],
                                 dev[:, hb], start=True, stop=True).then_inc(var_avg, 1)

            def passes(out, k, n, parts, hi_or_lo, start=False, stop=False):
                last = nc.tensor.matmul(out, w_block(HI, k, n), parts(hi_or_lo), start=start,
                                        stop=stop and hi_or_lo == LO, skip_group_check=True)
                if hi_or_lo == HI:
                    last = nc.tensor.matmul(out, w_block(LO, k, n), parts(HI), start=False, stop=False,
                                            skip_group_check=True)
                return last

            def input_products(k, s):
                first = is_first(s)

                def x_parts(part):
                    store = x_col if k == 2 else x_rows[:, :, line(k, s), :, :]
                    return store[:, part, :, :].rearrange("p b l -> p (b l)")

                ahead(pe, s, x_parts(HI), x_parts(LO))
                if k == 2:
                    pe.wait_ge(x_col_done, s + 1)
                if not first:
                    pe.wait_ge(sig_done[k], s)
                for gate in range(2):
                    out = rz_bank[k][:, gate * COLS:(gate + 1) * COLS]
                    passes(out, k, gate, x_parts, HI, start=gate == 0)
                    last = passes(out, k, gate, x_parts, LO, stop=first and gate == 1)
                if first:
                    last.then_inc(rz_ready[k], 1)
                else:
                    pe.wait_ge(npre_done[k], s)
                passes(n_bank[k][:, 0:COLS], k, 2, x_parts, HI, start=True)
                last = passes(n_bank[k][:, 0:COLS], k, 2, x_parts, LO, stop=first)
                if first:
                    last.then_inc(n_ready[k], 1)

            def hidden_products(k, s):
                def parts(part):
                    return h_parts[k][:, part, :]

                pe.wait_ge(h_hi_done[k], s)
                for gate in range(2):
                    passes(rz_bank[k][:, gate * COLS:(gate + 1) * COLS], k, GATES + gate, parts, HI)
                pe.wait_ge(h_lo_done[k], s)
                for gate in range(2):
                    last = passes(rz_bank[k][:, gate * COLS:(gate + 1) * COLS], k, GATES + gate, parts, LO,
                                  stop=gate == 1)
                last.then_inc(rz_ready[k], 1)
                passes(n_bank[k][:, COLS:2 * COLS], k, GATES + 2, parts, HI)
                passes(n_bank[k][:, COLS:2 * COLS], k, GATES + 2, parts, LO, stop=True) \
                    .then_inc(n_ready[k], 1)

            def convolution(k, s):
                out = conv_bank[k % 2][:, 0:COLS].rearrange("p (b l) -> p b l", b=B)

                def tap_lines(part, tap):
                    return ctx_store[k][:, part, line(k, s), :, tap:tap + LINE]

                ahead(pe, s + 1, *(tap_lines(part, tap) for part in (HI, LO) for tap in range(TAPS)))
                pe.wait_ge(ctx_hi_done[k], s + 1)
                if k == 2:
                    pe.wait_ge(h_done[0], s + 1)
                elif not is_first(s):
                    pe.wait_ge(h_done[1 if k == 1 else 2], s)
                for part in (HI, LO):
                    if part == LO:
                        pe.wait_ge(ctx_lo_done[k], s + 1)
                    for tap in range(TAPS):
                        last = passes(out, k, 2 * GATES + tap,
                                      lambda p: tap_lines(p, tap), part, start=part == HI and tap == 0, stop=tap == TAPS - 1)
                last.then_inc(conv_ready[k], 1)

            def steps(t, j):
                k, s = lagged(t, j, 2)
                if exists(s, STEPS - 2):
                    convolution(k, s)
                k, s = lagged(t, j, 0)
                if exists(s) and not is_first(s):
                    hidden_products(k, s)
                k, s = lagged(t, j, -1)
                if exists(s):
                    input_products(k, s)

            pe.wait_ge(w_lo_done, SETS)
            pe.wait_ge(x_lo_pool, POOL_IMAGES)
            pe.wait_ge(x_lo_dve, B - POOL_IMAGES)
            pe.wait_ge(var_eps, 2)
            input_products(0, 0)
            blocks(pe, steps)

            def chunk_part(c, k, start, stop):
                b, part = divmod(c, CHUNKS_B)
                rows = slice(part * CHUNK_ROWS, (part + 1) * CHUNK_ROWS)
                out = y_bank[c % RING][:].rearrange("p (h w) -> p h w", h=CHUNK_ROWS)

                def ctx_part(p):
                    if k == 2:
                        cells = slice(1 + part * CHUNK_ROWS, 1 + (part + 1) * CHUNK_ROWS)
                        return ctx_store[2][:, p, :, b, cells].rearrange("p w h -> p h w")
                    return ctx_store[k][:, p, rows, b, 1:1 + LINE]

                wk = DIRS * DIR_BLOCKS + k
                nc.tensor.matmul(out, w_parts[:, HI, wk, :], ctx_part(HI), start=start, stop=False,
                                 skip_group_check=True)
                nc.tensor.matmul(out, w_parts[:, LO, wk, :], ctx_part(HI), start=False, stop=False,
                                 skip_group_check=True)
                return nc.tensor.matmul(out, w_parts[:, HI, wk, :], ctx_part(LO), start=False, stop=stop,
                                        skip_group_check=True)

            for k in range(DIRS - 1):
                pe.wait_ge(ctx_lo_done[k], STEPS)
            for c0 in range(0, B * CHUNKS_B, RING):
                for c in range(c0, c0 + RING):
                    if c >= RING:
                        pe.wait_ge(y_biased, c - RING + 1)
                    chunk_part(c, 0, True, False)
                    chunk_part(c, 1, False, False)
                if c0 == 0:
                    pe.wait_ge(ctx_lo_done[2], STEPS)
                for c in range(c0, c0 + RING):
                    chunk_part(c, 2, False, True).then_inc(y_ready, 1)


def _weight_sets():
    sets = []
    for k in range(DIRS):
        conv = k * DIR_BLOCKS + 2 * GATES
        sets += [(k, k * DIR_BLOCKS, conv), (DIRS + k, conv, (k + 1) * DIR_BLOCKS)]
    return sets + [(2 * DIRS, DIRS * DIR_BLOCKS, BLOCKS)]


WEIGHT_SETS = _weight_sets()
POW_BEFORE = (0, 4)
POOL_IMAGES = 3


def kernel(**inputs):
    import numpy as np
    import concourse.bacc as bacc
    from concourse.bass_utils import run_bass_kernel_spmd

    blocks = []
    for d in ("d", "u", "r"):
        blocks.append(np.asarray(inputs[f"L0_conv_wih_{d}"]).T)
        blocks.append(np.asarray(inputs[f"L0_conv_whh_{d}"]).T)
        blocks.append(np.asarray(inputs[f"L0_conv_cw_{d}"]).transpose(1, 2, 0).reshape(C, TAPS * C))
    blocks.append(np.asarray(inputs["L0_conv_w_comb"]).T.reshape(DIRS + 1, C, C)[:DIRS]
                  .transpose(1, 0, 2).reshape(C, DIRS * C))
    arrays = {
        "x": np.ascontiguousarray(inputs["x"]),
        "weights": np.ascontiguousarray(np.concatenate(blocks, axis=1)),
        "biases": np.ascontiguousarray(np.stack(
            [np.asarray(inputs[n]) for n in ("L0_conv_cb_d", "L0_conv_cb_u", "L0_conv_cb_r", "L0_conv_b_comb")],
            axis=1)),
    }
    nc = bacc.Bacc("TRN2", target_bir_lowering=False, num_devices=1)
    aps = [nc.dram_tensor(f"{n}_dram", a.shape, mybir.dt.from_np(a.dtype), kind="ExternalInput").ap()
           for n, a in arrays.items()]
    out = nc.dram_tensor("out_dram", (B, C, H, W), mybir.dt.float32, kind="ExternalOutput").ap()
    build(nc, *aps, out)
    return run_bass_kernel_spmd(nc, [{f"{n}_dram": a for n, a in arrays.items()}], core_ids=[0]).results[0]["out_dram"]
```

```python
import concourse.bass as bass
import concourse.mybir as mybir

B, C, H, W = 8, 128, 32, 32
GROUPS = 32
GROUP_C = C // GROUPS
LINE = W
STEPS = H
COLS = B * LINE
PAD = LINE + 2
SPACE = H * W
DIRS = 3
GATES = 3
TAPS = 3
DIR_BLOCKS = 2 * GATES + TAPS
BLOCKS = DIRS + DIRS * DIR_BLOCKS
SETS = 2 * DIRS + 1
EPS = 1e-5
ACT_SCALE = 512.0
W_TOP = 2.0 ** 14
LEAST_SUM = 2.0 ** -100
HI, LO = 0, 1
COMB = DIRS
OUT_COLS = 512
CHUNK_ROWS = OUT_COLS // W
CHUNKS_B = SPACE // OUT_COLS
RING = 4
COMB_SET = SETS - 1
BATCHES = ((0, 3), (3, 7), (7, 8))
ACT_IMAGES = (0, 1, 3)
DVE_IMAGES = (2, 4, 5, 6, 7)
POOL_IMAGES = 2
EDGE = 4
LAST_COLS = 2
WHOLE_IMAGES = 3
REST_HI_IN_BLOCK = {(0, 0): (4,), (0, 1): (5, 6), (0, 2): (7,)}
REST_LO_AHEAD = 3
REST_LO_IN_BLOCK = {(0, 0): (3,), (0, 1): (4, 5), (0, 2): (6,), (1, 0): (7,)}
WARM_PRODUCTS = 8


def build(nc, x_d, w_d, bias_d, out_d):
    from contextlib import ExitStack
    f32, f16, i32 = mybir.dt.float32, mybir.dt.float16, mybir.dt.int32
    ALU, ACT = mybir.AluOpType, mybir.ActivationFunctionType

    with ExitStack() as ctx:
        def sb(name, shape, dt):
            return ctx.enter_context(nc.sbuf_tensor(name, shape, dt))

        def sem(name):
            return ctx.enter_context(nc.semaphore(name))

        def per_dir(name):
            return [sem(f"{name}_{k}") for k in range(DIRS)]

        ctx_store = [sb(f"ctx_store_{k}", [C, 2, STEPS, B, PAD], f16) for k in range(DIRS)]
        x_rows = sb("x_rows", [C, 2, H, B, W], f16)
        x_col = sb("x_col", [C, 2, B, H], f16)
        x32 = sb("x32", [C, B, H, W], f32)
        w_parts = sb("w_parts", [C, 2, BLOCKS, C], f16)
        rz = [sb(f"rz_{k}", [C, 2, COLS], f32) for k in range(DIRS)]
        npre = [sb(f"npre_{k}", [C, COLS], f32) for k in range(DIRS)]
        nval = [sb(f"nval_{k}", [C, COLS], f32) for k in range(DIRS)]
        hval = [sb(f"hval_{k}", [C, COLS], f32) for k in range(DIRS)]
        context = [sb(f"context_{k}", [C, B, PAD], f32) for k in range(DIRS)]
        h_parts = [sb(f"h_parts_{k}", [C, 2, COLS], f16) for k in range(DIRS)]
        biases = sb("biases", [C, DIRS + 1], f32)
        abs_sum = sb("abs_sum", [C, SETS], f32)
        allsum = sb("allsum", [C, SETS], f32)
        pow2 = sb("pow2", [C, SETS], f32)
        w_scale = sb("w_scale", [C, SETS], f32)
        descale = sb("descale", [C, SETS], f32)
        first_sigmoid = sb("first_sigmoid", [C, 1], f32)
        group_avg = sb("group_avg", [C, C], f32)
        stats = sb("stats", [C, B, CHUNKS_B, 6], f32)
        meanvar = sb("meanvar", [C, B, 2], f32)
        gmean = sb("gmean", [C, B], f32)
        dev = sb("dev", [C, B], f32)
        gvar = sb("gvar", [C, B], f32)
        minus_half = sb("minus_half", [C, B], f32)
        inv_std = sb("inv_std", [C, B], f32)
        x_scale = sb("x_scale", [C, B], f32)
        x_shift = sb("x_shift", [C, B], f32)
        def two_images(k, part):
            lines = slice(STEPS // 2, STEPS) if k == 0 else slice(0, STEPS // 2)
            return ctx_store[k][:, part, lines, :, :].rearrange("p t b l -> p (t b l)")[:, 0:4 * SPACE] \
                .bitcast(f32).rearrange("p (i h w) -> p i h w", i=2, h=H)

        x_norm = [two_images(k, part)[:, i, :, :] for k in (0, 2) for part in range(2) for i in range(2)]
        w32 = ctx_store[1][:].rearrange("p a t b l -> p (a t b l)")[:, 0:2 * BLOCKS * C] \
            .bitcast(f32).rearrange("p (n c) -> p n c", n=BLOCKS)
        magnitudes = ctx_store[2][:].rearrange("p a t b l -> p (a t b l)")[:, 0:2 * BLOCKS * C] \
            .bitcast(f32).rearrange("p (n c) -> p n c", n=BLOCKS)
        y_sb = x_rows[:].rearrange("p a h b w -> p (a h b w)").bitcast(f32) \
            .rearrange("p (n s) -> p n s", n=B * CHUNKS_B)

        def bank(name):
            return ctx.enter_context(nc.psum_tensor(name, [C, 512], f32))

        rz_bank = [bank(f"rz_bank_{k}") for k in range(DIRS)]
        n_bank = [bank(f"n_bank_{k}") for k in range(DIRS)]
        conv_bank = [bank(f"conv_bank_{i}") for i in range(2)]
        y_bank = [rz_bank[0], n_bank[0], rz_bank[1], n_bank[1]]
        avg_bank = [conv_bank[0], conv_bank[1], n_bank[2]]

        w_loaded = [sem(f"w_loaded_{k}") for k in range(DIRS + 1)]
        bias_loaded = sem("bias_loaded")
        x_loaded = [sem(f"x_loaded_{b}") for b in range(B)]
        pool_built = sem("pool_built")
        sides_zero = sem("sides_zero")
        stats_done = sem("stats_done")
        aggr_done = sem("aggr_done")
        mean_avg = sem("mean_avg")
        dve_chain = sem("dve_chain")
        spread_done = sem("spread_done")
        var_avg = sem("var_avg")
        var_eps = sem("var_eps")
        pow_done = sem("pow_done")
        x_factor = sem("x_factor")
        x_normed = sem("x_normed")
        x_normed_act = sem("x_normed_act")
        x_hi_done = sem("x_hi_done")
        x_lo_pool = sem("x_lo_pool")
        x_lo_dve = sem("x_lo_dve")
        rest_hi_done = sem("rest_hi_done")
        rest_lo_done = sem("rest_lo_done")
        x_col_done = sem("x_col_done")
        sum_done = sem("sum_done")
        allsum_done = sem("allsum_done")
        scale_done = sem("scale_done")
        w_scaled = sem("w_scaled")
        w_hi_done = sem("w_hi_done")
        w_lo_done = sem("w_lo_done")
        rz_ready = per_dir("rz_ready")
        n_ready = per_dir("n_ready")
        conv_ready = per_dir("conv_ready")
        sig_done = per_dir("sig_done")
        rh_done = per_dir("rh_done")
        npre_done = per_dir("npre_done")
        n_done = per_dir("n_done")
        zn_done = per_dir("zn_done")
        ctx_done = per_dir("ctx_done")
        ctx_hi_done = per_dir("ctx_hi_done")
        ctx_lo_done = per_dir("ctx_lo_done")
        h_done = per_dir("h_done")
        h_hi_done = per_dir("h_hi_done")
        h_lo_done = per_dir("h_lo_done")
        y_ready = sem("y_ready")
        x_biased = sem("x_biased")
        y_summed = sem("y_summed")
        y_stored = sem("y_stored")

        def line(k, step):
            return step if k == 0 else step * -1 + (STEPS - 1)

        def lagged(t, j, lag):
            return (j - lag) % DIRS, t + (j - lag) // DIRS

        def exists(step, last=STEPS - 1):
            return not isinstance(step, int) or 0 <= step <= last

        def is_first(step):
            return isinstance(step, int) and step == 0

        def blocks(eng, block):
            for t in (0, 1):
                for j in range(DIRS):
                    block(t, j)
            with eng.Fori(2, STEPS - 1) as t:
                for j in range(DIRS):
                    block(t, j)
            for t in (STEPS - 1, STEPS):
                for j in range(DIRS):
                    block(t, j)

        def ahead(eng, *operands):
            for x in operands:
                if isinstance(x, int):
                    continue
                if isinstance(x, bass.AP):
                    eng.lower_ap(x)
                else:
                    eng.compute_val(x)

        def context_lines(k, s, part):
            return ctx_store[k][:, part, line(k, s), :, :].rearrange("p b l -> p (b l)")

        def w_block(part, k, n):
            return w_parts[:, part, DIRS + k * DIR_BLOCKS + n, :]

        def gate_scale(k):
            return descale[:, k:k + 1]

        def residual(c):
            b, part = divmod(c, CHUNKS_B)
            return x32[:, b, part * CHUNK_ROWS:(part + 1) * CHUNK_ROWS, :].rearrange("p h w -> p (h w)")

        def conv_scale(k):
            return descale[:, DIRS + k:DIRS + k + 1]

        def edge_rows(ap):
            return ap.rearrange("p (g r) w -> p g r w", r=EDGE)[:, 0:H // EDGE:H // EDGE - 1, :, :]

        def last_columns(ap):
            return ap[:, EDGE:H - EDGE, W - LAST_COLS:W]

        def rest(ap):
            return ap[:, EDGE:H - EDGE, 0:W - LAST_COLS]

        block = ctx.enter_context(nc.Block())

        @block.sync
        def _(sp):
            for k in list(range(DIRS)) + [COMB]:
                lo, hi = (DIRS + k * DIR_BLOCKS, DIRS + (k + 1) * DIR_BLOCKS) if k != COMB else (0, DIRS)
                sp.dma_start(w32[:, lo:hi, :], w_d[:, lo * C:hi * C].rearrange("p (n c) -> p n c", c=C)) \
                    .then_inc(w_loaded[k], 16)
            for b in range(B):
                sp.dma_start(x32[:, b, :, :], x_d[b, :, :, :]).then_inc(x_loaded[b], 16)
            sp.dma_start(biases[:], bias_d).then_inc(bias_loaded, 16)
            for c in range(B * CHUNKS_B):
                b, part = divmod(c, CHUNKS_B)
                sp.wait_ge(y_summed, c + 1)
                sp.dma_start(out_d[b, :, part * CHUNK_ROWS:(part + 1) * CHUNK_ROWS, :]
                             .rearrange("c h w -> c (h w)"), y_sb[:, c, :]) \
                    .then_inc(y_stored, 16)
            sp.wait_ge(y_stored, 16 * B * CHUNKS_B)

        @block.gpsimd
        def _(pool):
            nc.gpsimd.memset(minus_half[:], -0.5)
            nc.gpsimd.memset(group_avg[:], 1.0 / GROUP_C).then_inc(pool_built, 1)
            groups = group_avg[:].rearrange("p (g c) -> p g c", g=GROUPS)
            pool.wait_ge(pool_built, 1)
            nc.gpsimd.affine_select(out=groups, in_=groups, compare_op=ALU.is_ge, fill=0.0, base=0,
                                    pattern=[[-GROUP_C, GROUPS], [0, GROUP_C]],
                                    channel_multiplier=1).then_inc(pool_built, 1)
            pool.wait_ge(pool_built, 2)
            nc.gpsimd.affine_select(out=groups, in_=groups, compare_op=ALU.is_ge, fill=0.0,
                                    base=GROUP_C - 1, pattern=[[GROUP_C, GROUPS], [0, GROUP_C]],
                                    channel_multiplier=-1).then_inc(pool_built, 1)
            for k in range(DIRS):
                nc.gpsimd.memset(context[k][:, :, 0:PAD:PAD - 1], 0.0).then_inc(sides_zero, 1)
            pool.wait_ge(sum_done, SETS)
            nc.gpsimd.partition_all_reduce(allsum[:], abs_sum[:], C, bass.bass_isa.ReduceOp.max) \
                .then_inc(allsum_done, 1)

            def inverse_deviation(n):
                first, end = BATCHES[n]
                pool.wait_ge(var_eps, n + 1)
                nc.gpsimd.tensor_tensor(out=inv_std[:, first:end], in0=gvar[:, first:end],
                                        in1=minus_half[:, first:end], op=ALU.pow).then_inc(pow_done, 1)

            def weights_lo(s):
                _, lo, hi = WEIGHT_SETS[s]
                pool.wait_ge(w_hi_done, s + 1)
                nc.gpsimd.tensor_tensor(out=w_parts[:, LO, lo:hi, :], in0=w32[:, lo:hi, :],
                                        in1=w_parts[:, HI, lo:hi, :], op=ALU.subtract) \
                    .then_inc(w_lo_done, 1)

            def x_lo(b):
                pool.wait_ge(x_hi_done, b + 1)
                for cells in (edge_rows, last_columns):
                    nc.gpsimd.tensor_tensor(out=cells(x_rows[:, LO, :, b, :]), in0=cells(x_norm[b]),
                                            in1=cells(x_rows[:, HI, :, b, :]),
                                            op=ALU.subtract).then_inc(x_lo_pool, 1)

            weights_lo(0)
            weights_lo(1)
            inverse_deviation(0)
            for s in range(2, COMB_SET):
                weights_lo(s)
            for b in range(POOL_IMAGES):
                x_lo(b)
            inverse_deviation(1)
            inverse_deviation(2)
            pool.wait_ge(rest_lo_done, B)
            weights_lo(COMB_SET)

        @block.scalar
        def _(act):
            act.wait_ge(pool_built, 1)
            nc.scalar.activation(first_sigmoid[:], minus_half[:, 0:1], ACT.Sigmoid)
            for k in range(DIRS + 1):
                act.wait_ge(w_loaded[k], 16)
                for n, lo, hi in WEIGHT_SETS[2 * k:2 * k + 2]:
                    nc.scalar.activation(magnitudes[:, lo:hi, :], w32[:, lo:hi, :], ACT.Abs,
                                         accum_out=abs_sum[:, n:n + 1]).then_inc(sum_done, 1)
            act.wait_ge(scale_done, 1)

            def scale_weights(s):
                n, lo, hi = WEIGHT_SETS[s]
                nc.scalar.activation(w32[:, lo:hi, :], w32[:, lo:hi, :], ACT.Copy,
                                     scale=w_scale[:, n:n + 1]).then_inc(w_scaled, 1)

            def weights_hi(s):
                _, lo, hi = WEIGHT_SETS[s]
                act.wait_ge(w_scaled, s + 1)
                nc.scalar.activation(w_parts[:, HI, lo:hi, :], w32[:, lo:hi, :], ACT.Copy) \
                    .then_inc(w_hi_done, 1)

            def normalise(b):
                act.wait_ge(x_factor, 1 if b < BATCHES[0][1] else 2)
                nc.scalar.activation(x_norm[b], x32[:, b, :, :], ACT.Identity,
                                     bias=x_shift[:, b:b + 1], scale=x_scale[:, b:b + 1]) \
                    .then_inc(x_normed_act, 1)

            def rest_hi(b):
                nc.scalar.activation(rest(x_rows[:, HI, :, b, :]), rest(x_norm[b]), ACT.Copy) \
                    .then_inc(rest_hi_done, 1)

            def image_hi(b):
                if b in ACT_IMAGES:
                    act.wait_ge(x_normed_act, ACT_IMAGES.index(b) + 1)
                else:
                    act.wait_ge(x_normed, DVE_IMAGES.index(b) + 1)
                if b < WHOLE_IMAGES:
                    nc.scalar.activation(x_rows[:, HI, :, b, :], x_norm[b], ACT.Copy).then_inc(x_hi_done, 1)
                else:
                    nc.scalar.activation(edge_rows(x_rows[:, HI, :, b, :]), edge_rows(x_norm[b]), ACT.Copy)
                    nc.scalar.activation(last_columns(x_rows[:, HI, :, b, :]), last_columns(x_norm[b]),
                                         ACT.Copy).then_inc(x_hi_done, 1)

            scale_weights(0)
            for s in range(COMB_SET):
                if s + 1 < COMB_SET:
                    scale_weights(s + 1)
                else:
                    normalise(0)
                weights_hi(s)
            normalise(1)
            for b in range(WHOLE_IMAGES):
                image_hi(b)
            scale_weights(COMB_SET)
            weights_hi(COMB_SET)
            normalise(3)
            for b in range(WHOLE_IMAGES, B):
                image_hi(b)
            rest_hi(WHOLE_IMAGES)
            act.wait_ge(bias_loaded, 16)
            act.wait_ge(x_lo_pool, 2 * POOL_IMAGES)
            act.wait_ge(x_lo_dve, 2 * (B - POOL_IMAGES))
            act.wait_ge(sides_zero, DIRS)

            def column(s):
                nc.scalar.activation(x_col[:], x_rows[:, :, :, :, line(2, s)].rearrange("p a h b -> p a b h"),
                                     ACT.Copy).then_inc(x_col_done, 1)

            def gates(k, s):
                act.wait_ge(rz_ready[k], s + 1)
                nc.scalar.activation(rz[k][:].rearrange("p g c -> p (g c)"), rz_bank[k][:],
                                     ACT.Sigmoid, scale=gate_scale(k)).then_inc(sig_done[k], 1)

            def new_value(k, s):
                if is_first(s):
                    act.wait_ge(n_ready[k], 1)
                    nc.scalar.activation(nval[k][:], n_bank[k][:, 0:COLS], ACT.Tanh,
                                         scale=gate_scale(k)).then_inc(n_done[k], 1)
                else:
                    act.wait_ge(npre_done[k], s)
                    nc.scalar.activation(nval[k][:], npre[k][:], ACT.Tanh).then_inc(n_done[k], 1)

            def hidden(k, s):
                act.wait_ge(conv_ready[k], s + 1)
                nc.scalar.activation(hval[k][:], conv_bank[k % 2][:, 0:COLS], ACT.Tanh,
                                     bias=biases[:, k:k + 1], scale=conv_scale(k)).then_inc(h_done[k], 1)

            def context_hi(k, s):
                act.wait_ge(ctx_done[k], s + 1)
                nc.scalar.activation(context_lines(k, s, HI), context[k][:].rearrange("p b l -> p (b l)"),
                                     ACT.Copy, scale=ACT_SCALE).then_inc(ctx_hi_done[k], 1)

            def hidden_hi(k, s):
                act.wait_ge(h_done[k], s + 1)
                nc.scalar.activation(h_parts[k][:, HI, :], hval[k][:], ACT.Copy, scale=ACT_SCALE) \
                    .then_inc(h_hi_done[k], 1)

            def steps(t, j):
                now, nxt, before = lagged(t, j, 0), lagged(t, j, -1), lagged(t, j, 1)
                starting = is_first(t)
                if exists(now[1]):
                    ahead(act, now[1], now[1] + 1, line(*now) * (B * PAD))
                    new_value(*now)
                if exists(before[1], STEPS - 2) and not starting:
                    hidden(*before)
                if exists(nxt[1]):
                    gates(*nxt)
                for b in REST_HI_IN_BLOCK.get((t, j), ()) if isinstance(t, int) else ():
                    rest_hi(b)
                if exists(now[1]):
                    context_hi(*now)
                if exists(before[1], STEPS - 2):
                    if starting:
                        hidden(*before)
                    hidden_hi(*before)
                if j == DIRS - 1 and exists(t + 1):
                    if isinstance(t, int) and t == 1:
                        act.wait_ge(w_lo_done, SETS)
                        act.wait_ge(rest_lo_done, B)
                    column(t + 1)

            column(0)
            gates(0, 0)
            blocks(act, steps)

            for c in range(B * CHUNKS_B):
                nc.scalar.activation(residual(c), residual(c), ACT.Identity,
                                     bias=biases[:, DIRS:DIRS + 1]).then_inc(x_biased, 1)

        @block.vector
        def _(dve):
            chained = [0]

            def chain(instruction):
                chained[0] += 1
                instruction.then_inc(dve_chain, 1)
                dve.wait_ge(dve_chain, chained[0])

            def image_stats(b):
                dve.wait_ge(x_loaded[b], 16)
                for i in range(CHUNKS_B):
                    rows = slice(i * CHUNK_ROWS, (i + 1) * CHUNK_ROWS)
                    nc.vector.bn_stats(out=stats[:, b, i, :],
                                       in_=x32[:, b, rows, :].rearrange("p h w -> p (h w)")) \
                        .then_inc(stats_done, 1)
                dve.wait_ge(stats_done, CHUNKS_B * (b + 1))
                nc.vector.bn_aggr(out=meanvar[:, b, :], in_=stats[:, b, :, :].rearrange("p i s -> p (i s)")) \
                    .then_inc(aggr_done, 1)

            def spread(n):
                ims = slice(*BATCHES[n])
                dve.wait_ge(mean_avg, n + 1)
                chain(nc.vector.tensor_copy(gmean[:, ims], avg_bank[n][:, ims]))
                chain(nc.vector.tensor_tensor(out=dev[:, ims], in0=meanvar[:, ims, 0], in1=gmean[:, ims],
                                              op=ALU.subtract))
                chain(nc.vector.tensor_tensor(out=dev[:, ims], in0=dev[:, ims], in1=dev[:, ims], op=ALU.mult))
                nc.vector.tensor_tensor(out=dev[:, ims], in0=dev[:, ims], in1=meanvar[:, ims, 1],
                                        op=ALU.add).then_inc(spread_done, 1)

            def variance(n):
                first, end = BATCHES[n]
                dve.wait_ge(var_avg, n + 1)
                nc.vector.tensor_scalar(gvar[:, first:end], avg_bank[n][:, B + first:B + end], EPS, None,
                                        ALU.add).then_inc(var_eps, 1)

            def factor(n):
                ims = slice(*BATCHES[n])
                dve.wait_ge(pow_done, n + 1)
                chain(nc.vector.tensor_scalar(x_scale[:, ims], inv_std[:, ims], ACT_SCALE, None, ALU.mult))

            def shift(n):
                ims = slice(*BATCHES[n])
                nc.vector.scalar_tensor_tensor(x_shift[:, ims], gmean[:, ims], -1.0, x_scale[:, ims],
                                               ALU.mult, ALU.mult).then_inc(x_factor, 1)

            def normalise(b):
                nc.vector.tensor_scalar(x_norm[b].rearrange("p h w -> p (h w)"),
                                        x32[:, b, :, :].rearrange("p h w -> p (h w)"),
                                        gmean[:, b:b + 1], x_scale[:, b:b + 1],
                                        ALU.subtract, ALU.mult).then_inc(x_normed, 1)

            def x_lo(b):
                dve.wait_ge(x_hi_done, b + 1)
                for cells in (edge_rows, last_columns):
                    nc.vector.tensor_tensor(out=cells(x_rows[:, LO, :, b, :]), in0=cells(x_norm[b]),
                                            in1=cells(x_rows[:, HI, :, b, :]),
                                            op=ALU.subtract).then_inc(x_lo_dve, 1)

            def rest_lo(b):
                if b >= WHOLE_IMAGES:
                    dve.wait_ge(rest_hi_done, b - WHOLE_IMAGES + 1)
                nc.vector.tensor_tensor(out=rest(x_rows[:, LO, :, b, :]), in0=rest(x_norm[b]),
                                        in1=rest(x_rows[:, HI, :, b, :]),
                                        op=ALU.subtract).then_inc(rest_lo_done, 1)

            def weight_scales():
                dve.wait_ge(allsum_done, 1)
                chain(nc.vector.tensor_scalar(allsum[:], allsum[:], LEAST_SUM, None, ALU.max))
                chain(nc.vector.tensor_scalar(pow2[:].bitcast(i32), allsum[:].bitcast(i32), 0x7F800000, None,
                                              ALU.bitwise_and))
                chain(nc.vector.tensor_scalar(descale[:], pow2[:], 1.0 / (W_TOP * ACT_SCALE), None, ALU.mult))
                chain(nc.vector.reciprocal(w_scale[:], pow2[:]))
                nc.vector.tensor_scalar(w_scale[:], w_scale[:], W_TOP, None, ALU.mult).then_inc(scale_done, 1)

            image_stats(0)
            weight_scales()
            image_stats(1)
            image_stats(2)
            spread(0)
            image_stats(3)
            variance(0)
            image_stats(4)
            factor(0)
            shift(0)
            image_stats(5)
            image_stats(6)
            normalise(2)
            spread(1)
            image_stats(7)
            variance(1)
            x_lo(2)
            spread(2)
            factor(1)
            shift(1)
            normalise(4)
            variance(2)
            normalise(5)
            normalise(6)
            factor(2)
            normalise(7)
            for b in range(3, B):
                x_lo(b)
            for b in range(REST_LO_AHEAD):
                rest_lo(b)

            def lines(ap):
                return ap.rearrange("p (b l) -> p b l", b=B)

            def blend(k, s):
                zh, z = rz[k][:, 0, :], rz[k][:, 1, :]
                dve.wait_ge(n_done[k], s + 1)
                if is_first(s):
                    dve.wait_ge(sig_done[k], 1)
                nc.vector.scalar_tensor_tensor(nval[k][:], z, 1.0, nval[k][:], ALU.subtract,
                                               ALU.mult).then_inc(zn_done[k], 1)
                dve.wait_ge(zn_done[k], s + 1)
                if is_first(s):
                    nc.vector.tensor_scalar(context[k][:, :, 1:1 + LINE], lines(nval[k][:]), -1.0, None,
                                            ALU.mult).then_inc(ctx_done[k], 1)
                else:
                    nc.vector.tensor_tensor(out=context[k][:, :, 1:1 + LINE], in0=lines(zh),
                                            in1=lines(nval[k][:]), op=ALU.subtract).then_inc(ctx_done[k], 1)

            def reset_hidden(k, s):
                dve.wait_ge(sig_done[k], s + 1)
                dve.wait_ge(n_ready[k], s + 1)
                nc.vector.scalar_tensor_tensor(npre[k][:], n_bank[k][:, COLS:2 * COLS], gate_scale(k),
                                               rz[k][:, 0, :], ALU.mult, ALU.mult).then_inc(rh_done[k], 1)

            def context_lo(k, s):
                dve.wait_ge(ctx_hi_done[k], s + 1)
                nc.vector.scalar_tensor_tensor(
                    context_lines(k, s, LO), context[k][:].rearrange("p b l -> p (b l)"), ACT_SCALE,
                    context_lines(k, s, HI), ALU.mult, ALU.subtract).then_inc(ctx_lo_done[k], 1)

            def tanh_argument(k, s):
                dve.wait_ge(rh_done[k], s)
                nc.vector.scalar_tensor_tensor(npre[k][:], n_bank[k][:, 0:COLS], gate_scale(k),
                                               npre[k][:], ALU.mult, ALU.add).then_inc(npre_done[k], 1)

            def hidden_lo(k, s):
                dve.wait_ge(h_hi_done[k], s + 1)
                nc.vector.scalar_tensor_tensor(h_parts[k][:, LO, :], hval[k][:], ACT_SCALE,
                                               h_parts[k][:, HI, :], ALU.mult,
                                               ALU.subtract).then_inc(h_lo_done[k], 1)

            def z_times_h(k):
                nc.vector.tensor_tensor(out=rz[k][:, 0, :], in0=rz[k][:, 1, :], in1=hval[k][:], op=ALU.mult)

            def steps(t, j):
                now, nxt, before = lagged(t, j, 0), lagged(t, j, -1), lagged(t, j, 1)
                if exists(now[1]):
                    ahead(dve, now[1] + 1, context_lines(*now, HI), context_lines(*now, LO))
                    blend(*now)
                if exists(nxt[1]) and not is_first(nxt[1]):
                    reset_hidden(*nxt)
                if exists(now[1]):
                    for b in REST_LO_IN_BLOCK.get((t, j), ()) if isinstance(t, int) else ():
                        rest_lo(b)
                    context_lo(*now)
                if exists(nxt[1]) and not is_first(nxt[1]):
                    tanh_argument(*nxt)
                if exists(before[1], STEPS - 2):
                    hidden_lo(*before)
                if exists(nxt[1]) and not is_first(nxt[1]):
                    z_times_h(nxt[0])

            dve.wait_ge(sides_zero, DIRS)
            blocks(dve, steps)

            for c in range(B * CHUNKS_B):
                dve.wait_ge(y_ready, c + 1)
                dve.wait_ge(x_biased, c + 1)
                nc.vector.scalar_tensor_tensor(y_sb[:, c, :], y_bank[c % RING][:],
                                               descale[:, 2 * DIRS:2 * DIRS + 1], residual(c),
                                               ALU.mult, ALU.add).then_inc(y_summed, 1)

        @block.tensor
        def _(pe):
            pe.wait_ge(pool_built, 3)
            for n, (first, end) in enumerate(BATCHES):
                pe.wait_ge(aggr_done, end)
                nc.tensor.matmul(avg_bank[n][:, first:end], group_avg[:], meanvar[:, first:end, 0],
                                 start=True, stop=True).then_inc(mean_avg, 1)
                pe.wait_ge(spread_done, n + 1)
                nc.tensor.matmul(avg_bank[n][:, B + first:B + end], group_avg[:], dev[:, first:end],
                                 start=True, stop=True).then_inc(var_avg, 1)

            def passes(out, k, n, parts, hi_or_lo, start=False, stop=False):
                last = nc.tensor.matmul(out, w_block(HI, k, n), parts(hi_or_lo), start=start,
                                        stop=stop and hi_or_lo == LO, skip_group_check=True)
                if hi_or_lo == HI:
                    last = nc.tensor.matmul(out, w_block(LO, k, n), parts(HI), start=False, stop=False,
                                            skip_group_check=True)
                return last

            def input_products(k, s):
                first = is_first(s)

                def x_parts(part):
                    store = x_col if k == 2 else x_rows[:, :, line(k, s), :, :]
                    return store[:, part, :, :].rearrange("p b l -> p (b l)")

                ahead(pe, s, x_parts(HI), x_parts(LO))
                if k == 2:
                    pe.wait_ge(x_col_done, s + 1)
                if not first:
                    pe.wait_ge(sig_done[k], s)
                for gate in range(2):
                    out = rz_bank[k][:, gate * COLS:(gate + 1) * COLS]
                    passes(out, k, gate, x_parts, HI, start=gate == 0)
                    last = passes(out, k, gate, x_parts, LO, stop=first and gate == 1)
                if first:
                    last.then_inc(rz_ready[k], 1)
                elif isinstance(s, int) and s == 1:
                    pe.wait_ge(n_done[k], 1)
                else:
                    pe.wait_ge(npre_done[k], s - 1)
                passes(n_bank[k][:, 0:COLS], k, 2, x_parts, HI, start=True)
                last = passes(n_bank[k][:, 0:COLS], k, 2, x_parts, LO, stop=first)
                if first:
                    last.then_inc(n_ready[k], 1)

            def hidden_products(k, s):
                def parts(part):
                    return h_parts[k][:, part, :]

                pe.wait_ge(h_hi_done[k], s)
                for gate in range(2):
                    passes(rz_bank[k][:, gate * COLS:(gate + 1) * COLS], k, GATES + gate, parts, HI)
                pe.wait_ge(h_lo_done[k], s)
                for gate in range(2):
                    last = passes(rz_bank[k][:, gate * COLS:(gate + 1) * COLS], k, GATES + gate, parts, LO,
                                  stop=gate == 1)
                last.then_inc(rz_ready[k], 1)
                passes(n_bank[k][:, COLS:2 * COLS], k, GATES + 2, parts, HI)
                passes(n_bank[k][:, COLS:2 * COLS], k, GATES + 2, parts, LO, stop=True) \
                    .then_inc(n_ready[k], 1)

            def convolution(k, s):
                out = conv_bank[k % 2][:, 0:COLS].rearrange("p (b l) -> p b l", b=B)

                def tap_lines(part, tap):
                    return ctx_store[k][:, part, line(k, s), :, tap:tap + LINE]

                ahead(pe, s + 1, *(tap_lines(part, tap) for part in (HI, LO) for tap in range(TAPS)))
                pe.wait_ge(ctx_hi_done[k], s + 1)
                if k == 2:
                    pe.wait_ge(h_done[0], s + 1)
                elif not is_first(s):
                    pe.wait_ge(h_done[1 if k == 1 else 2], s)
                for part in (HI, LO):
                    if part == LO:
                        pe.wait_ge(ctx_lo_done[k], s + 1)
                    for tap in range(TAPS):
                        last = passes(out, k, 2 * GATES + tap,
                                      lambda p: tap_lines(p, tap), part,
                                      start=part == HI and tap == 0, stop=tap == TAPS - 1)
                last.then_inc(conv_ready[k], 1)

            def chunk_part(c, k):
                b, part = divmod(c, CHUNKS_B)
                rows = slice(part * CHUNK_ROWS, (part + 1) * CHUNK_ROWS)
                out = y_bank[c % RING][:].rearrange("p (h w) -> p h w", h=CHUNK_ROWS)

                def ctx_part(p):
                    if k == 2:
                        cells = slice(1 + part * CHUNK_ROWS, 1 + (part + 1) * CHUNK_ROWS)
                        return ctx_store[2][:, p, :, b, cells].rearrange("p w h -> p h w")
                    return ctx_store[k][:, p, rows, b, 1:1 + LINE]

                nc.tensor.matmul(out, w_parts[:, HI, k, :], ctx_part(HI), start=k == 0, stop=False,
                                 skip_group_check=True)
                nc.tensor.matmul(out, w_parts[:, LO, k, :], ctx_part(HI), start=False, stop=False,
                                 skip_group_check=True)
                return nc.tensor.matmul(out, w_parts[:, HI, k, :], ctx_part(LO), start=False,
                                        stop=k == DIRS - 1, skip_group_check=True)

            def steps(t, j):
                k, s = lagged(t, j, 2)
                if exists(s, STEPS - 2):
                    convolution(k, s)
                if j == 2 and isinstance(t, int) and t == STEPS - 1:
                    pe.wait_ge(w_lo_done, SETS)
                    pe.wait_ge(npre_done[0], STEPS - 1)
                    pe.wait_ge(ctx_lo_done[0], STEPS)
                    for c in (0, 1):
                        chunk_part(c, 0)
                k, s = lagged(t, j, 0)
                if exists(s) and not is_first(s):
                    hidden_products(k, s)
                if isinstance(t, int) and (t, j) == (1, 2):
                    pe.wait_ge(rest_lo_done, B)
                k, s = lagged(t, j, -1)
                if exists(s):
                    input_products(k, s)

            pe.wait_ge(w_lo_done, COMB_SET)
            for _ in range(WARM_PRODUCTS):
                nc.tensor.matmul(rz_bank[2][:], w_block(HI, 0, 0),
                                 w_parts[:, HI, DIRS:DIRS + OUT_COLS // C, :].rearrange("p n c -> p (n c)"),
                                 start=True, stop=True, skip_group_check=True)
            pe.wait_ge(x_lo_pool, 2 * POOL_IMAGES)
            pe.wait_ge(x_lo_dve, 2 * (B - POOL_IMAGES))
            pe.wait_ge(var_eps, len(BATCHES))
            input_products(0, 0)
            blocks(pe, steps)

            pe.wait_ge(npre_done[1], STEPS - 1)
            for c in (2, 3):
                chunk_part(c, 0)
            pe.wait_ge(ctx_lo_done[1], STEPS)
            for c in range(RING):
                chunk_part(c, 1)
            pe.wait_ge(ctx_lo_done[2], STEPS)
            for c in range(RING):
                chunk_part(c, 2).then_inc(y_ready, 1)
            for c in range(RING, B * CHUNKS_B):
                pe.wait_ge(y_summed, c - RING + 1)
                for k in range(DIRS):
                    last = chunk_part(c, k)
                last.then_inc(y_ready, 1)


def _weight_sets():
    sets = []
    for k in range(DIRS):
        first = DIRS + k * DIR_BLOCKS
        conv = first + 2 * GATES
        sets += [(k, first, conv), (DIRS + k, conv, first + DIR_BLOCKS)]
    return sets + [(2 * DIRS, 0, DIRS)]


WEIGHT_SETS = _weight_sets()


def kernel(**inputs):
    import numpy as np
    import concourse.bacc as bacc
    from concourse.bass_utils import run_bass_kernel_spmd

    blocks = [np.asarray(inputs["L0_conv_w_comb"]).T.reshape(DIRS + 1, C, C)[:DIRS]
              .transpose(1, 0, 2).reshape(C, DIRS * C)]
    for d in ("d", "u", "r"):
        blocks.append(np.asarray(inputs[f"L0_conv_wih_{d}"]).T)
        blocks.append(np.asarray(inputs[f"L0_conv_whh_{d}"]).T)
        blocks.append(np.asarray(inputs[f"L0_conv_cw_{d}"]).transpose(1, 2, 0).reshape(C, TAPS * C))
    arrays = {
        "x": np.ascontiguousarray(inputs["x"]),
        "weights": np.ascontiguousarray(np.concatenate(blocks, axis=1)),
        "biases": np.ascontiguousarray(np.stack(
            [np.asarray(inputs[n]) for n in ("L0_conv_cb_d", "L0_conv_cb_u", "L0_conv_cb_r", "L0_conv_b_comb")],
            axis=1)),
    }
    nc = bacc.Bacc("TRN2", target_bir_lowering=False, num_devices=1)
    aps = [nc.dram_tensor(f"{n}_dram", a.shape, mybir.dt.from_np(a.dtype), kind="ExternalInput").ap()
           for n, a in arrays.items()]
    out = nc.dram_tensor("out_dram", (B, C, H, W), mybir.dt.float32, kind="ExternalOutput").ap()
    build(nc, *aps, out)
    return run_bass_kernel_spmd(nc, [{f"{n}_dram": a for n, a in arrays.items()}], core_ids=[0]).results[0]["out_dram"]
```
